# Optimizing a Trainium2 kernel written in Bass

```python
import numpy as np
import jax
import jax.numpy as jnp

def _softmax(x, axis=-1):
    return jax.nn.softmax(x, axis=axis)

def _gelu(x):
    return jax.nn.gelu(x, approximate=True)

def _silu(x):
    return jax.nn.silu(x)

def _sigmoid(x):
    return jax.nn.sigmoid(x)

def _layernorm(x, axis=-1, eps=1e-05):
    m = jnp.mean(x, axis=axis, keepdims=True)
    v = jnp.var(x, axis=axis, keepdims=True)
    return (x - m) / jnp.sqrt(v + eps)

def _scatter_add(tgt, idx, src, axis=0):
    return tgt.at[idx].add(src)

def _segment_sum(src, seg, n):
    return jax.ops.segment_sum(src, seg, n)
kernel_name = 'mk_perceiver_d1_seqx_r8_258498'

def setup_inputs(seed: int=0):
    np.random.seed(seed)
    _w = jnp.asarray

    def _rec_inputs():
        import jax
        import jax.numpy as jnp
        _rk = jax.random.key(seed)
        x = -0.000125 + 0.9999 * jax.random.normal(jax.random.fold_in(_rk, 1), (2, 128, 256), jnp.float32)
        _lenS = 128 - jax.random.randint(jax.random.fold_in(_rk, 7), (2,), 0, max(1, 128 // 4) + 1, jnp.int32)
        _lenS2 = 2048 - jax.random.randint(jax.random.fold_in(_rk, 8), (2,), 0, max(1, 2048 // 4) + 1, jnp.int32)
        _ctx_2048P = jax.random.normal(jax.random.fold_in(_rk, 11), (2, 16, 256), jnp.float32)
        _ctx_2048c = jax.random.dirichlet(jax.random.fold_in(_rk, 511), 0.3 * jnp.ones((16,), jnp.float32), (2, 2048))
        _ctx_2048t = jnp.einsum('bsk,bkd->bsd', _ctx_2048c, _ctx_2048P)
        _ctx_2048t = _ctx_2048t * jax.lax.rsqrt(jnp.mean(jnp.square(_ctx_2048t)) + 1e-12) * 0.953939
        ctx_2048 = -0.000514642 + 1.00011 * (_ctx_2048t + 0.3 * jax.random.normal(jax.random.fold_in(_rk, 611), (2, 2048, 256), jnp.float32))
        _validS = jnp.arange(128)[None, :] < _lenS[:, None]
        _validS2 = jnp.arange(2048)[None, :] < _lenS2[:, None]
        _causal = jnp.tril(jnp.ones((128, 128), dtype=bool))
        mask_BxS2_bk0 = jnp.logical_not(jnp.broadcast_to(_validS2[:, :], (2, 2048)))
        return (x, ctx_2048, mask_BxS2_bk0)
    x, ctx_2048, mask_BxS2_bk0 = _rec_inputs()

    def _L0_xattn_setup():
        import jax, jax.numpy as jnp
        import numpy as np
        key = jax.random.key(seed)
        k1, k2, k3 = jax.random.split(key, 3)
        B, S, D, M = (8, 256, 256, 128)
        hidden_states = jax.random.normal(k1, (B, S, D), dtype=jnp.float32)
        memory_tokens = jax.random.normal(k2, (B, M, D), dtype=jnp.float32)
        memory_mask = jax.random.randint(k3, (B, M), 0, 2).astype(jnp.bool_)
        return {'hidden_states': hidden_states, 'memory_tokens': memory_tokens, 'memory_mask': memory_mask}
    _L0_xattn_all = _L0_xattn_setup()
    _L0_xattn_in = {k: v for k, v in _L0_xattn_all.items() if k in ()}
    del _L0_xattn_all

    def _L0_attn_setup():
        import jax, jax.numpy as jnp
        import numpy as np
        BATCH, SEQ, HID, INTER, NSTATE, DTRANK, KCONV = (1, 128, 256, 512, 16, 128, 4)
        EPS = 1e-06

        def _rms(x):
            x32 = x.astype(jnp.float32)
            return (x32 * jax.lax.rsqrt(jnp.mean(x32 * x32, axis=-1, keepdims=True) + EPS)).astype(x.dtype)
        key = jax.random.key(seed)
        ks = jax.random.split(key, 8)
        x = jax.random.normal(ks[0], (BATCH, SEQ, HID), jnp.float32)
        in_proj_w = jax.random.normal(ks[1], (HID, 2 * INTER), jnp.float32) * 0.02
        conv_w = jax.random.normal(ks[2], (INTER, 1, KCONV), jnp.float32) * 0.2
        conv_b = jnp.zeros((INTER,), jnp.float32)
        x_proj_w = jax.random.normal(ks[3], (INTER, DTRANK + 2 * NSTATE), jnp.float32) * 0.02
        dt_proj_w = jax.random.normal(ks[4], (DTRANK, INTER), jnp.float32) * DTRANK ** (-0.5)
        dt_proj_b = jax.random.normal(ks[5], (INTER,), jnp.float32) * 0.1
        out_proj_w = jax.random.normal(ks[6], (INTER, HID), jnp.float32) * 0.02
        A_log = jnp.log(jnp.broadcast_to(jnp.arange(1, NSTATE + 1, dtype=jnp.float32), (INTER, NSTATE)))
        D_param = jnp.ones((INTER,), jnp.float32)
        return {'x': x, 'in_proj_w': in_proj_w, 'conv_w': conv_w, 'conv_b': conv_b, 'x_proj_w': x_proj_w, 'dt_proj_w': dt_proj_w, 'dt_proj_b': dt_proj_b, 'out_proj_w': out_proj_w, 'A_log': A_log, 'D_param': D_param}
    _L0_attn_all = _L0_attn_setup()
    _L0_attn_in = {k: v for k, v in _L0_attn_all.items() if k in ('in_proj_w', 'conv_w', 'conv_b', 'x_proj_w', 'dt_proj_w', 'dt_proj_b', 'out_proj_w', 'A_log', 'D_param')}
    del _L0_attn_all

    def _L0_ffn_setup():
        import jax, jax.numpy as jnp
        import numpy as np
        from jax import lax
        H = 256
        I = 176
        E = 16
        TOP_K = 6
        IS = 2 * I

        def _swiglu(x, w13_, w2_):
            gu = x @ w13_.T
            g, u = jnp.split(gu, 2, axis=-1)
            return jax.nn.silu(g) * u @ w2_.T
        key = jax.random.key(seed)
        ks = jax.random.split(key, 6)
        return {'hidden_states': jax.random.normal(ks[0], (1, 256, H), jnp.float32), 'gate_w': jax.random.normal(ks[1], (E, H), jnp.float32) * 0.02, 'w13': jax.random.normal(ks[2], (E, 2 * I, H), jnp.float32) * 0.02, 'w2': jax.random.normal(ks[3], (E, H, I), jnp.float32) * 0.02, 'sw13': jax.random.normal(ks[4], (2 * IS, H), jnp.float32) * 0.02, 'sw2': jax.random.normal(ks[5], (H, IS), jnp.float32) * 0.02}
    _L0_ffn_all = _L0_ffn_setup()
    _L0_ffn_in = {k: v for k, v in _L0_ffn_all.items() if k in ('gate_w', 'w13', 'w2', 'sw13', 'sw2')}
    del _L0_ffn_all
    return {'x': x, 'ctx_2048': ctx_2048, 'mask_BxS2_bk0': mask_BxS2_bk0, 'L0_attn_in_proj_w': _L0_attn_in['in_proj_w'], 'L0_attn_conv_w': _L0_attn_in['conv_w'], 'L0_attn_conv_b': _L0_attn_in['conv_b'], 'L0_attn_x_proj_w': _L0_attn_in['x_proj_w'], 'L0_attn_dt_proj_w': _L0_attn_in['dt_proj_w'], 'L0_attn_dt_proj_b': _L0_attn_in['dt_proj_b'], 'L0_attn_out_proj_w': _L0_attn_in['out_proj_w'], 'L0_attn_A_log': _L0_attn_in['A_log'], 'L0_attn_D_param': _L0_attn_in['D_param'], 'L0_ffn_gate_w': _L0_ffn_in['gate_w'], 'L0_ffn_w13': _L0_ffn_in['w13'], 'L0_ffn_w2': _L0_ffn_in['w2'], 'L0_ffn_sw13': _L0_ffn_in['sw13'], 'L0_ffn_sw2': _L0_ffn_in['sw2']}

def reference(x, ctx_2048, mask_BxS2_bk0, L0_attn_in_proj_w, L0_attn_conv_w, L0_attn_conv_b, L0_attn_x_proj_w, L0_attn_dt_proj_w, L0_attn_dt_proj_b, L0_attn_out_proj_w, L0_attn_A_log, L0_attn_D_param, L0_ffn_gate_w, L0_ffn_w13, L0_ffn_w2, L0_ffn_sw13, L0_ffn_sw2):
    import jax
    import jax.numpy as jnp

    def _L0_xattn_ref(hidden_states, memory_tokens, memory_mask):
        import jax, jax.numpy as jnp
        import numpy as np
        B, S, D = hidden_states.shape
        scale = 1.0 / jnp.sqrt(jnp.asarray(D, hidden_states.dtype))
        scores = jnp.einsum('bsd,bmd->bsm', hidden_states, memory_tokens) * scale
        neg_inf = jnp.asarray(-1e+30, scores.dtype)
        scores = jnp.where(memory_mask[:, None, :], scores, neg_inf)
        attn = jax.nn.softmax(scores, axis=-1)
        readout = jnp.einsum('bsm,bmd->bsd', attn, memory_tokens)
        valid_b = jnp.any(memory_mask, axis=-1)
        out = jnp.where(valid_b[:, None, None], readout, jnp.zeros_like(readout))
        return out

    def _L0_attn_ref(x, in_proj_w, conv_w, conv_b, x_proj_w, dt_proj_w, dt_proj_b, out_proj_w, A_log, D_param):
        import jax, jax.numpy as jnp
        import numpy as np
        BATCH, SEQ, HID, INTER, NSTATE, DTRANK, KCONV = (1, 128, 256, 512, 16, 128, 4)
        EPS = 1e-06

        def _rms(x):
            x32 = x.astype(jnp.float32)
            return (x32 * jax.lax.rsqrt(jnp.mean(x32 * x32, axis=-1, keepdims=True) + EPS)).astype(x.dtype)
        Bsz, L, _ = x.shape
        proj = x @ in_proj_w
        hidden, gate = jnp.split(proj, 2, axis=-1)
        h = jnp.swapaxes(hidden, 1, 2)
        h = jax.lax.conv_general_dilated(h, conv_w, window_strides=(1,), padding=((KCONV - 1, KCONV - 1),), feature_group_count=INTER)[..., :L]
        h = h + conv_b[None, :, None]
        hs = jnp.swapaxes(jax.nn.silu(h), 1, 2)
        ssm_p = hs @ x_proj_w
        dt, Bm, Cm = jnp.split(ssm_p, [DTRANK, DTRANK + NSTATE], axis=-1)
        Bm, Cm, dt = (_rms(Bm), _rms(Cm), _rms(dt))
        dt = jax.nn.softplus(dt @ dt_proj_w + dt_proj_b)
        A = -jnp.exp(A_log.astype(jnp.float32))
        dt32 = dt.astype(jnp.float32)
        u = hs.astype(jnp.float32)
        dA = jnp.exp(dt32[..., None] * A)
        dBu = (dt32 * u)[..., None] * Bm.astype(jnp.float32)[:, :, None, :]
        C32 = Cm.astype(jnp.float32)

        def step(s, inp):
            dA_t, dBu_t, C_t = inp
            s = dA_t * s + dBu_t
            y = jnp.einsum('bdn,bn->bd', s, C_t)
            return (s, y)
        s0 = jnp.zeros((Bsz, INTER, NSTATE), jnp.float32)
        _, ys = jax.lax.scan(step, s0, (jnp.swapaxes(dA, 0, 1), jnp.swapaxes(dBu, 0, 1), jnp.swapaxes(C32, 0, 1)))
        y = jnp.swapaxes(ys, 0, 1)
        y = y + u * D_param
        y = y * jax.nn.silu(gate)
        return y.astype(x.dtype) @ out_proj_w

    def _L0_ffn_ref(hidden_states, gate_w, w13, w2, sw13, sw2):
        import jax, jax.numpy as jnp
        import numpy as np
        from jax import lax
        H = 256
        I = 176
        E = 16
        TOP_K = 6
        IS = 2 * I

        def _swiglu(x, w13_, w2_):
            gu = x @ w13_.T
            g, u = jnp.split(gu, 2, axis=-1)
            return jax.nn.silu(g) * u @ w2_.T
        B, S, Hd = hidden_states.shape
        x = hidden_states.reshape(-1, Hd)
        T = x.shape[0]
        scores = jax.nn.softmax(x @ gate_w.T, axis=-1)
        topk_w, topk_ids = lax.top_k(scores, TOP_K)
        topk_w = topk_w / (topk_w.sum(-1, keepdims=True) + 1e-20)
        combine = jnp.einsum('tk,tke->te', topk_w, jax.nn.one_hot(topk_ids, E, dtype=topk_w.dtype))

        def body(acc, ew):
            w13_e, w2_e, c_e = ew
            y = _swiglu(x, w13_e, w2_e)
            return (acc + c_e[:, None] * y, None)
        out, _ = lax.scan(body, jnp.zeros_like(x), (w13, w2, combine.T))
        out = out + _swiglu(x, sw13, sw2)
        return out.reshape(B, S, Hd)
    x = x + _L0_xattn_ref(_layernorm(x, axis=-1), ctx_2048, mask_BxS2_bk0)
    x = x + _L0_attn_ref(_layernorm(x, axis=-1), L0_attn_in_proj_w, L0_attn_conv_w, L0_attn_conv_b, L0_attn_x_proj_w, L0_attn_dt_proj_w, L0_attn_dt_proj_b, L0_attn_out_proj_w, L0_attn_A_log, L0_attn_D_param)
    x = x + _L0_ffn_ref(_layernorm(x, axis=-1), L0_ffn_gate_w, L0_ffn_w13, L0_ffn_w2, L0_ffn_sw13, L0_ffn_sw2)
    return x

_drawn_inputs = setup_inputs


def setup_inputs(seed=0):
    import zlib

    import numpy as np

    out = dict(_drawn_inputs(seed))
    spreads = {'L0_attn_conv_b': (0.0, 0.463), 'L0_attn_D_param': (1.0, 0.6)}
    factors = {'L0_attn_in_proj_w': 2.999,
     'L0_attn_conv_w': 2.986,
     'L0_attn_x_proj_w': 3.006,
     'L0_attn_dt_proj_w': 5.729,
     'L0_attn_dt_proj_b': 8.0,
     'L0_attn_out_proj_w': 2.932,
     'L0_attn_A_log': 8.0,
     'L0_ffn_gate_w': 8.0,
     'L0_ffn_w13': 8.0,
     'L0_ffn_w2': 8.0,
     'L0_ffn_sw13': 3.274,
     'L0_ffn_sw2': 3.295}
    for name, (base, spread) in spreads.items():
        noise = np.random.default_rng([zlib.crc32(name.encode()), seed]).standard_normal(out[name].shape)
        drawn = base * np.exp(spread * noise) if base else spread * noise
        out[name] = jnp.asarray(drawn.astype(out[name].dtype))
    for name, factor in factors.items():
        out[name] = (out[name] * factor).astype(out[name].dtype)
    return out
```

```python
from contextlib import ExitStack

import concourse.bass as bass
from concourse import mybir

F32 = mybir.dt.float32
BF16 = mybir.dt.bfloat16
U8 = mybir.dt.uint8
ALU = mybir.AluOpType
ACT = mybir.ActivationFunctionType
AX = mybir.AxisListType


def build(nc, x, ctx_t, ctx_n, mask, in_w, chan, x_w, dt_w, out_w, gate_w, w13, w2, out):
    P = 128
    B, T, D = x.shape
    KEYS = ctx_n.shape[1]
    KD = D // P
    KB = KEYS // 512
    C = out_w.shape[0]
    CT = C // P
    R = dt_w.shape[0]
    N = (x_w.shape[1] - R) // 2
    TAPS = 4
    E = gate_w.shape[1]
    PAIRS = w13.shape[0]
    I = w13.shape[3] // 2
    TOPK = 6
    HC = [(0, P), (P, P), (2 * P, 2 * I - 2 * P)]
    SCALE = float(D) ** -0.5
    LN_EPS, RMS_EPS = 1e-5, 1e-6
    MASKED = -1e30
    NBC = 2 * N * T // 512

    with ExitStack() as ctx:
        def sb(name, shape, dt=F32):
            return ctx.enter_context(nc.sbuf_tensor(name, shape, dt))

        def psum(name, shape, dt=F32):
            return ctx.enter_context(nc.psum_tensor(name, shape, dt))

        def sem(name):
            return ctx.enter_context(nc.semaphore(name))

        work = psum("work", [P, 4, 512])
        tr_ps = psum("tr_ps", [P, 512])
        xt_ps = psum("xt_ps", [P, 512])
        tok_ps = psum("tok_ps", [P, 512])
        acc_ps = psum("acc_ps", [P, 512])
        ro_ps = tok_ps[:, 0:D]
        op_ps = tok_ps[:, D:2 * D]
        lg_ps = xt_ps[:, 256:256 + E]

        w13_len = PAIRS * KD * 4 * I
        w2_len = PAIRS * 3 * D
        big = sb("big", [P, w13_len + w2_len])
        ctx_len = KD * KEYS

        def ctxT_sb(b):
            return big[:, 2 * b * ctx_len:(2 * b + 1) * ctx_len].rearrange("p (c k) -> p c k", c=KD)

        def ctxN_sb(b):
            return big[:, (2 * b + 1) * ctx_len:(2 * b + 2) * ctx_len].rearrange("p (c d) -> p c d", d=D)

        def w13_sb(p):
            n = KD * 4 * I
            return big[:, p * n:(p + 1) * n].rearrange("p (c e i) -> p c e i", c=KD, e=2)

        def w2_off(p):
            return w13_len + (PAIRS - 1 - p) * 3 * D

        def w2_sb(p):
            return big[:, w2_off(p):w2_off(p) + 3 * D].rearrange("p (c d) -> p c d", c=3)

        inw_sb = sb("inw_sb", [P, KD, 2 * C])
        xw_sb = sb("xw_sb", [P, CT, R + 2 * N])
        dtw_sb = sb("dtw_sb", [P, C])
        outw_sb = sb("outw_sb", [P, CT, D])
        gw_sb = sb("gw_sb", [P, KD, E])
        NCH = TAPS + 3 + N
        chan_sb = sb("chan_sb", [P, CT, NCH])
        half_sb = sb("half_sb", [P, CT, TAPS + 1])
        negA_sb = sb("negA_sb", [P, CT, N])
        ones_bf = sb("ones_bf", [1, P], BF16)
        ident = sb("ident", [P, P])
        ident_bf = sb("ident_bf", [P, P], BF16)
        pick = sb("pick", [3 * 2 * N, 2 * N], BF16)
        tmp_pick = sb("tmp_pick", [3 * 2 * N, 2 * N])
        neghalf = sb("neghalf", [P, 3])

        x_sb = sb("x_sb", [P, B, D])
        x1_sb = sb("x1_sb", [P, B, D])
        x2_sb = sb("x2_sb", [P, B, D])
        fin_sb = x1_sb
        stats = sb("stats", [P, B, 3, 6])
        mv = sb("mv", [P, B, 3, 2])
        ve = sb("ve", [P, B, 3])
        rstd = sb("rstd", [P, B, 3])
        xn_sb = sb("xn_sb", [P, B, D])
        xT_sb = sb("xT_sb", [P, B, KD, T])

        probs = sb("probs", [P, 2, KEYS])
        p_sb = probs[:, 0, :]
        pT_sb = probs[:, 1, :].rearrange("p (c t) -> p c t", t=T)
        bc0 = sb("bc0", [P, 2 * N * T])
        bc_sb = [bc0[:, :], probs[:, :, :].rearrange("p a k -> p (a k)")]
        mx4 = sb("mx4", [P, B, KB])
        mx = sb("mx", [P, B])
        nm = sb("nm", [P, B])
        valid = sb("valid", [P, B])
        sum4 = sb("sum4", [P, B, KB])
        rsum = sb("rsum", [P, B])
        rinv = sb("rinv", [P, B])
        rvalid = sb("rvalid", [P, B])

        hpad = sb("hpad", [P, CT, T + TAPS - 1])
        cg = sb("cg", [P, CT, T])
        th = sb("th", [P, CT, T])
        thg = sb("thg", [P, CT, T])
        z_sb = sb("z_sb", [P, CT, T])
        u_sb = sb("u_sb", [P, B, CT, T])
        sg_sb = sb("sg_sb", [P, B, CT, T])
        dt_sb = sb("dt_sb", [P, B, CT, T])
        dtu_sb = sb("dtu_sb", [P, B, CT, T])
        ss = sb("ss", [P, B, 3])
        sse = sb("sse", [P, B, 3])
        rr = sb("rr", [P, B, 3])
        dtn = sb("dtn", [P, R])
        dtT = sb("dtT", [P, T])
        bcn = sb("bcn", [P, 2, N])
        bcr = sb("bcr", [P, 2, N])
        parts = sb("parts", [P, 3, 2, N], BF16)
        partsT = sb("partsT", [3 * 2 * N, T], BF16)

        dA = sb("dA", [P, 2, N, T])
        st = sb("st", [P, 2, N, T])
        mask_u8 = st[0:1, 0].rearrange("p n t -> p (n t)")[:, 0:B * KEYS // 4].bitcast(U8)
        y_sb = sb("y_sb", [P, T])
        y2_sb = sb("y2_sb", [P, T])

        ffn_buf = sb("ffn_buf", [P, 8 * I + 6 * P])
        tg = ffn_buf[:, 0:4 * I].rearrange("p (k i) -> p k i", k=4)
        h_sb = ffn_buf[:, 4 * I:8 * I].rearrange("p (k i) -> p k i", k=2)
        hT = ffn_buf[:, 8 * I:8 * I + 6 * P].rearrange("p (k c) -> p k c", k=2)
        mask_sb = ffn_buf[0:1, 0:B * KEYS // 2].bitcast(BF16)
        nlg = sb("nlg", [P, B])
        ex = sb("ex", [P, E])
        exs = sb("exs", [P, 1])
        exr = sb("exr", [P, 1])
        sc = sb("sc", [P, E + 2])
        rep = sb("rep", [P, E + 2])
        v8 = sb("v8", [P, 8])
        chosen = sb("chosen", [P, E])
        tks = sb("tks", [P, 1])
        tke = sb("tke", [P, 1])
        tkr = sb("tkr", [P, 1])
        cw = sb("cw", [P, B, E + 2])

        ld_x, ld_mask, ld_inw, ld_chan = sem("ld_x"), sem("ld_mask"), sem("ld_inw"), sem("ld_chan")
        ld_xw, ld_dtw, ld_outw, ld_gw = sem("ld_xw"), sem("ld_dtw"), sem("ld_outw"), sem("ld_gw")
        ld_ctxT = [[sem(f"ld_ctxT{b}{j}") for j in range(KB)] for b in range(B)]
        ld_ctxN = [[sem(f"ld_ctxN{b}{j}") for j in range(2)] for b in range(B)]
        ld_w13 = [sem(f"ld_w13_{p}") for p in range(PAIRS)]
        ld_w2 = [sem(f"ld_w2_{p}") for p in range(PAIRS)]
        stored = sem("stored")
        s = {}
        for name in """zeroed ident_ready ident_bf_ready pick_half pick_ready mask_ready ones_ready consts_ready
                half_ready A_exp A_ready pads_ready dA0_ready
                scores_ready max4_done max_done nm_ready valid_ready probs_ready pT_psum pT_act pT_dve
                readout_ready sum_done rinv_done rvalid_ready x1_ready
                h_ready gate_ready hpad_ready tap_act tap_done tanh_h u_ready tanh_g sg_ready
                xp_ready ss_ready sse_ready rr_ready dtn_ready bcn_ready part0 rest1 part1 part2
                dtT_psum dtT_ready partsT_psum partsT_ready z_psum z_ready abs_ready e_ready w_ready nc_ready
                ln_ready q_ready dt_ready dtu_ready bc_psum bcB_ready bcC_ready
                dA_ready dBu_ready scan_done mulC_done y_ready y2_ready yg_ready
                op_ready x2_ready
                lg_ready nlg_ready ex_ready exr_ready sc_ready v8_ready v8s_ready tks_ready rep_ready chosen_ready
                tke_ready tkr_ready cw_ready cw_const sentinel
                gu_ready tg_ready t1_ready hf_ready tr_ready hT_ready w2_done fin_ready""".split():
            s[name] = sem(name)
        bn_done = [sem(f"bn_done{l}") for l in range(3)]
        var_ready = [sem(f"var_ready{l}") for l in range(3)]
        ve_ready = [sem(f"ve_ready{l}") for l in range(3)]
        rstd_ready = [sem(f"rstd_ready{l}") for l in range(3)]
        xn_ready = [sem(f"xn_ready{l}") for l in range(3)]
        xT_psum = [sem(f"xT_psum{l}") for l in range(3)]
        xT_ready = [sem(f"xT_ready{l}") for l in range(3)]

        block = ctx.enter_context(nc.Block())

        @block.sync
        def _(sp):
            def load_ctx(b):
                src = ctx_t[b].rearrange("(c p) k -> p c k", p=P)
                for j in range(KB):
                    sp.dma_start(ctxT_sb(b)[:, :, j * 512:(j + 1) * 512],
                                 src[:, :, j * 512:(j + 1) * 512]).then_inc(ld_ctxT[b][j], 16)
                nat = ctx_n[b].rearrange("(c p) d -> p c d", p=P)
                half = KEYS // P // 2
                for j in range(2):
                    sp.dma_start(ctxN_sb(b)[:, j * half:(j + 1) * half, :],
                                 nat[:, j * half:(j + 1) * half, :]).then_inc(ld_ctxN[b][j], 16)

            sp.dma_start(x_sb[:, :, :], x.rearrange("b t d -> t b d")).then_inc(ld_x, 16)
            sp.dma_start(mask_u8[:, :], mask).then_inc(ld_mask, 16)
            load_ctx(0)
            sp.dma_start(inw_sb[:, :, :], in_w.rearrange("(c p) n -> p c n", p=P)).then_inc(ld_inw, 16)
            sp.dma_start(chan_sb[:, :, :], chan).then_inc(ld_chan, 16)
            sp.dma_start(xw_sb[:, :, :], x_w.rearrange("(c p) n -> p c n", p=P)).then_inc(ld_xw, 16)
            sp.dma_start(dtw_sb[:, :], dt_w).then_inc(ld_dtw, 16)
            load_ctx(1)
            sp.dma_start(outw_sb[:, :, :], out_w.rearrange("(c p) n -> p c n", p=P)).then_inc(ld_outw, 16)
            sp.dma_start(gw_sb[:, :, :], gate_w.rearrange("(c p) n -> p c n", p=P)).then_inc(ld_gw, 16)

            def load_w13(p):
                sp.dma_start(w13_sb(p), w13[p].rearrange("(c k) e i -> k c e i", k=P)).then_inc(ld_w13[p], 16)

            def load_w2(p):
                rows = w2[p * 2 * I:(p + 1) * 2 * I, :]
                sp.dma_start(w2_sb(p)[:, 0:2, :],
                             rows[0:2 * P, :].rearrange("(c k) d -> k c d", k=P)).then_inc(ld_w2[p], 16)
                sp.dma_start(w2_sb(p)[0:HC[2][1], 2, :], rows[2 * P:2 * I, :]).then_inc(ld_w2[p], 16)

            sp.wait_ge(s["readout_ready"], 1)
            n13 = KD * 4 * I
            early = [p for p in range(PAIRS) if (p + 1) * n13 <= 2 * ctx_len]
            early2 = [p for p in range(PAIRS) if w2_off(p) >= 4 * ctx_len]
            for p in early:
                load_w13(p)
                if p in early2:
                    load_w2(p)
            sp.wait_ge(s["readout_ready"], 2)
            for p in range(PAIRS):
                if p not in early:
                    load_w13(p)
                if p not in early2 or p not in early:
                    load_w2(p)
            for b in range(B):
                sp.wait_ge(s["fin_ready"], b + 1)
                sp.dma_start(out[b], fin_sb[:, b, :]).then_inc(stored, 16)
            sp.wait_ge(stored, 16 * B)

        @block.gpsimd
        def _(pool):
            g = nc.gpsimd
            g.memset(ident[:, :], 0.0).then_inc(s["zeroed"], 1)
            pool.wait_ge(s["zeroed"], 1)
            g.affine_select(out=ident[:, :], in_=ident[:, :], compare_op=ALU.not_equal, fill=1.0, base=0,
                            pattern=[[-1, P]], channel_multiplier=1).then_inc(s["ident_ready"], 1)
            g.memset(neghalf[:, :], -0.5).then_inc(s["consts_ready"], 1)
            pool.wait_ge(s["consts_ready"], 1)

            def rsqrt_var(l, b):
                pool.wait_ge(var_ready[l], b + 1)
                g.tensor_scalar(ve[:, b, l:l + 1], mv[:, b, l, 1:2], LN_EPS, None, ALU.add).then_inc(ve_ready[l], 1)
                pool.wait_ge(ve_ready[l], b + 1)
                g.tensor_tensor(rstd[:, b, l:l + 1], ve[:, b, l:l + 1], neghalf[:, 0:1],
                                ALU.pow).then_inc(rstd_ready[l], 1)

            def rsqrt_rms(b):
                pool.wait_ge(s["ss_ready"], 3 * (b + 1))
                g.tensor_scalar(sse[:, b, :], ss[:, b, :], RMS_EPS, None, ALU.add).then_inc(s["sse_ready"], 1)
                pool.wait_ge(s["sse_ready"], b + 1)
                g.tensor_tensor(rr[:, b, :], sse[:, b, :], neghalf[:, :], ALU.pow).then_inc(s["rr_ready"], 1)

            def inputs(b, i):
                if i == 0:
                    pool.wait_ge(s["dtu_ready"], b + 1)
                    pool.wait_ge(s["bcB_ready"], NBC // 2 * (b + 1))
                k = CT * b + i
                if k >= 2:
                    pool.wait_ge(s["y_ready"], k - 1)
                bm = bc_sb[b][:, 0:N * T].rearrange("p (n t) -> p n t", n=N)
                g.tensor_tensor(st[:, k % 2], bm, dtu_sb[:, b, i:i + 1, :].to_broadcast([P, N, T]),
                                ALU.mult).then_inc(s["dBu_ready"], 1)

            rsqrt_var(0, 0)
            rsqrt_var(0, 1)
            rsqrt_var(1, 0)
            rsqrt_rms(0)
            inputs(0, 0)
            inputs(0, 1)
            inputs(0, 2)
            rsqrt_var(1, 1)
            inputs(0, 3)
            rsqrt_rms(1)
            rsqrt_var(2, 0)
            for i in range(CT):
                inputs(1, i)
            rsqrt_var(2, 1)

        @block.scalar
        def _(act):
            a = nc.scalar

            def xT_copy(l, b):
                act.wait_ge(xT_psum[l], b + 1)
                a.copy(xT_sb[:, b].rearrange("p c t -> p (c t)"), xt_ps[:, 0:D]).then_inc(xT_ready[l], 1)

            def softmax_exp(b):
                act.wait_ge(s["nm_ready"], b + 1)
                for j in range(KB):
                    a.activation(p_sb[:, j * 512:(j + 1) * 512], work[:, j, :], ACT.Exp, bias=nm[:, b:b + 1],
                                 scale=SCALE, accum_out=sum4[:, b, j:j + 1]).then_inc(s["probs_ready"], 1)

            def pT_copy(b, j):
                act.wait_ge(s["pT_psum"], KB * b + j + 1)
                a.copy(probs[:, 1, j * 512:(j + 1) * 512], work[:, j, :]).then_inc(s["pT_act"], 1)

            def front(b):
                act.wait_ge(s["hpad_ready"], b + 1)
                act.wait_ge(s["half_ready"], 1)
                for i in range(CT):
                    a.activation(cg[:, i, :], hpad[:, i, TAPS - 1:], ACT.Identity,
                                 scale=half_sb[:, i, TAPS - 1:TAPS],
                                 bias=half_sb[:, i, TAPS:TAPS + 1]).then_inc(s["tap_act"], 1)
                act.wait_ge(s["gate_ready"], b + 1)
                a.activation(thg[:, :, :].rearrange("p c t -> p (c t)"), work[:, 1, :], ACT.Tanh,
                             scale=0.5).then_inc(s["tanh_g"], 1)
                act.wait_ge(s["tap_done"], (TAPS - 1) * CT * (b + 1))
                a.activation(th[:, :, :], cg[:, :, :], ACT.Tanh).then_inc(s["tanh_h"], 1)

            def squares(b):
                act.wait_ge(s["xp_ready"], b + 1)
                for k, (lo, n) in enumerate([(0, R), (R, N), (R + N, N)]):
                    a.activation(z_sb[:, 0, 0:n], work[:, 2, lo:lo + n], ACT.Square, scale=float(n) ** -0.5,
                                 accum_out=ss[:, b, k:k + 1]).then_inc(s["ss_ready"], 1)
                    act.wait_ge(s["ss_ready"], 3 * b + k + 1)

            def dt_side(b):
                act.wait_ge(s["dtT_psum"], b + 1)
                a.copy(dtT[:, :], work[:, 2, 256:256 + T]).then_inc(s["dtT_ready"], 1)

            def softplus(b):
                act.wait_ge(s["z_ready"], b + 1)
                a.activation(th[:, :, :], z_sb[:, :, :], ACT.Abs).then_inc(s["abs_ready"], 1)
                act.wait_ge(s["abs_ready"], b + 1)
                a.activation(thg[:, :, :], th[:, :, :], ACT.Exp, scale=-1.0).then_inc(s["e_ready"], 1)
                act.wait_ge(s["w_ready"], b + 1)
                a.activation(th[:, :, :], cg[:, :, :], ACT.Ln).then_inc(s["ln_ready"], 1)

            def c_copy(b, j):
                act.wait_ge(s["bc_psum"], NBC * b + NBC // 2 + j + 1)
                lo = (NBC // 2 + j) * 512
                a.copy(bc_sb[b][:, lo:lo + 512], work[:, j, :]).then_inc(s["bcC_ready"], 1)

            def decays(b, i):
                k = CT * b + i
                if i == 0:
                    act.wait_ge(s["dt_ready"], b + 1)
                if k >= 2:
                    act.wait_ge(s["scan_done"], k - 1)
                for n in range(N):
                    last = a.activation(dA[:, k % 2, n, 1:T], dt_sb[:, b, i, 1:T], ACT.Exp,
                                        scale=negA_sb[:, i, n:n + 1])
                last.then_inc(s["dA_ready"], 1)

            def gate_exp(b):
                act.wait_ge(s["nlg_ready"], b + 1)
                a.activation(ex[:, :], lg_ps, ACT.Exp, bias=nlg[:, b:b + 1],
                             accum_out=exs[:, :]).then_inc(s["ex_ready"], 1)

            def ffn_tanh(b, p):
                for e in range(2):
                    k = 2 * (PAIRS * b + p) + e
                    act.wait_ge(s["gu_ready"], k + 1)
                    if k >= 4:
                        act.wait_ge(s["hf_ready"], k - 3)
                    a.activation(tg[:, k % 4, :], work[:, k % 4, 0:I], ACT.Tanh, scale=0.5).then_inc(s["tg_ready"], 1)

            def hT_copy(b, p):
                k = PAIRS * b + p
                act.wait_ge(s["tr_ready"], k + 1)
                if k >= 2:
                    act.wait_ge(s["w2_done"], k - 1)
                a.copy(hT[:, k % 2, 0:2 * P], tr_ps[:, 0:2 * P]).then_inc(s["hT_ready"], 1)
                m = HC[2][1]
                a.copy(hT[0:m, k % 2, 2 * P:3 * P], tr_ps[0:m, 2 * P:3 * P]).then_inc(s["hT_ready"], 1)

            xT_copy(0, 0)
            softmax_exp(0)
            pT_copy(0, 0)
            pT_copy(0, 2)
            act.wait_ge(ld_chan, 16)
            a.activation(negA_sb[:, :, :], chan_sb[:, :, TAPS + 3:NCH], ACT.Exp).then_inc(s["A_exp"], 1)
            xT_copy(1, 0)
            front(0)
            squares(0)
            dt_side(0)
            softplus(0)
            act.wait_ge(s["A_ready"], 1)
            act.wait_ge(s["dA0_ready"], 2)
            decays(0, 0)
            for j in range(4):
                c_copy(0, j)
            xT_copy(0, 1)
            decays(0, 1)
            softmax_exp(1)
            pT_copy(1, 0)
            pT_copy(1, 2)
            xT_copy(1, 1)
            front(1)
            squares(1)
            decays(0, 2)
            dt_side(1)
            softplus(1)
            decays(0, 3)
            for j in range(4):
                c_copy(1, j)
            decays(1, 0)
            xT_copy(2, 0)
            gate_exp(0)
            decays(1, 1)
            ffn_tanh(0, 0)
            for p in range(1, PAIRS):
                ffn_tanh(0, p)
                hT_copy(0, p - 1)
                if p in (2, 5):
                    decays(1, 2 + p // 5)
            hT_copy(0, PAIRS - 1)
            xT_copy(2, 1)
            gate_exp(1)
            ffn_tanh(1, 0)
            for p in range(1, PAIRS):
                ffn_tanh(1, p)
                hT_copy(1, p - 1)
            hT_copy(1, PAIRS - 1)

        @block.vector
        def _(dve):
            v = nc.vector

            def ln_stats(l, b, src):
                v.bn_stats(stats[:, b, l, :], src).then_inc(bn_done[l], 1)
                dve.wait_ge(bn_done[l], b + 1)
                v.bn_aggr(mv[:, b, l, :], stats[:, b, l, :]).then_inc(var_ready[l], 1)

            def ln_apply(l, b, src):
                if l:
                    dve.wait_ge(xT_psum[l - 1], b + 1)
                dve.wait_ge(rstd_ready[l], b + 1)
                v.tensor_scalar(xn_sb[:, b, :], src, mv[:, b, l, 0:1], rstd[:, b, l:l + 1],
                                ALU.subtract, ALU.mult).then_inc(xn_ready[l], 1)

            def score_max(b):
                for j in range(KB):
                    dve.wait_ge(s["scores_ready"], KB * b + j + 1)
                    v.reduce_max(mx4[:, b, j:j + 1], work[:, j, :], AX.X).then_inc(s["max4_done"], 1)
                dve.wait_ge(s["max4_done"], KB * (b + 1))
                v.reduce_max(mx[:, b:b + 1], mx4[:, b, :], AX.X).then_inc(s["max_done"], 1)
                dve.wait_ge(s["max_done"], b + 1)
                v.tensor_scalar(nm[:, b:b + 1], mx[:, b:b + 1], -SCALE, None, ALU.mult).then_inc(s["nm_ready"], 1)
                v.tensor_scalar(valid[:, b:b + 1], mx[:, b:b + 1], 0.1 * MASKED, None,
                                ALU.is_gt).then_inc(s["valid_ready"], 1)

            def pT_copy(b, j):
                dve.wait_ge(s["pT_psum"], KB * b + j + 1)
                v.tensor_copy(probs[:, 1, j * 512:(j + 1) * 512], work[:, j, :]).then_inc(s["pT_dve"], 1)

            def attn_sums(b):
                dve.wait_ge(s["probs_ready"], KB * (b + 1))
                v.reduce_sum(rsum[:, b:b + 1], sum4[:, b, :], AX.X).then_inc(s["sum_done"], 1)
                dve.wait_ge(s["sum_done"], b + 1)
                v.reciprocal(rinv[:, b:b + 1], rsum[:, b:b + 1]).then_inc(s["rinv_done"], 1)
                dve.wait_ge(s["rinv_done"], b + 1)
                dve.wait_ge(s["valid_ready"], b + 1)
                v.tensor_tensor(rvalid[:, b:b + 1], rinv[:, b:b + 1], valid[:, b:b + 1],
                                ALU.mult).then_inc(s["rvalid_ready"], 1)

            def residual1(b):
                dve.wait_ge(s["readout_ready"], b + 1)
                dve.wait_ge(s["rvalid_ready"], b + 1)
                v.scalar_tensor_tensor(out=x1_sb[:, b, :], in0=ro_ps, scalar=rvalid[:, b:b + 1],
                                       in1=x_sb[:, b, :], op0=ALU.mult, op1=ALU.add).then_inc(s["x1_ready"], 1)
                dve.wait_ge(s["x1_ready"], b + 1)
                ln_stats(1, b, x1_sb[:, b, :])
                ln_apply(1, b, x1_sb[:, b, :])

            def conv(b):
                dve.wait_ge(s["h_ready"], b + 1)
                v.tensor_copy(hpad[:, :, TAPS - 1:], work[:, 0, :].rearrange("p (c t) -> p c t", c=CT))\
                    .then_inc(s["hpad_ready"], 1)
                dve.wait_ge(s["hpad_ready"], b + 1)
                dve.wait_ge(s["tap_act"], CT * (b + 1))
                for k in range(TAPS - 1):
                    for i in range(CT):
                        if k:
                            dve.wait_ge(s["tap_done"], CT * ((TAPS - 1) * b + k - 1) + i + 1)
                        v.scalar_tensor_tensor(out=cg[:, i, :], in0=hpad[:, i, k:k + T],
                                               scalar=half_sb[:, i, k:k + 1], in1=cg[:, i, :],
                                               op0=ALU.mult, op1=ALU.add).then_inc(s["tap_done"], 1)
                dve.wait_ge(s["tanh_g"], b + 1)
                v.scalar_tensor_tensor(out=sg_sb[:, b].rearrange("p c t -> p (c t)"),
                                       in0=thg[:, :, :].rearrange("p c t -> p (c t)"), scalar=1.0,
                                       in1=work[:, 1, :], op0=ALU.add, op1=ALU.mult).then_inc(s["sg_ready"], 1)
                dve.wait_ge(s["tanh_h"], b + 1)
                v.scalar_tensor_tensor(out=u_sb[:, b], in0=th[:, :, :], scalar=1.0, in1=cg[:, :, :],
                                       op0=ALU.add, op1=ALU.mult).then_inc(s["u_ready"], 1)

            def normed(b):
                dve.wait_ge(s["rr_ready"], b + 1)
                v.tensor_scalar(dtn[:, :], work[:, 2, 0:R], rr[:, b, 0:1], None, ALU.mult)\
                    .then_inc(s["dtn_ready"], 1)
                v.tensor_tensor(bcn[:, :, :], work[:, 2, R:R + 2 * N].rearrange("p (a n) -> p a n", a=2),
                                rr[:, b, 1:3].unsqueeze(2).to_broadcast([P, 2, N]),
                                ALU.mult).then_inc(s["bcn_ready"], 1)
                dve.wait_ge(s["bcn_ready"], b + 1)
                v.tensor_copy(parts[:, 0], bcn[:, :, :]).then_inc(s["part0"], 1)
                dve.wait_ge(s["part0"], b + 1)
                v.tensor_tensor(bcr[:, :, :], bcn[:, :, :], parts[:, 0], ALU.subtract).then_inc(s["rest1"], 1)
                dve.wait_ge(s["rest1"], b + 1)
                v.tensor_copy(parts[:, 1], bcr[:, :, :]).then_inc(s["part1"], 1)
                dve.wait_ge(s["part1"], b + 1)
                v.tensor_tensor(parts[:, 2], bcr[:, :, :], parts[:, 1], ALU.subtract).then_inc(s["part2"], 1)

            def partsT_copy(b):
                dve.wait_ge(s["partsT_psum"], b + 1)
                v.tensor_copy(partsT[:, :], tr_ps[0:6 * N, 0:T // 2].bitcast(BF16)).then_inc(s["partsT_ready"], 1)

            def dt_bias(b):
                dve.wait_ge(s["z_psum"], b + 1)
                v.tensor_tensor(z_sb[:, :, :], work[:, 3, :].rearrange("p (c t) -> p c t", c=CT),
                                chan_sb[:, :, TAPS + 1:TAPS + 2].to_broadcast([P, CT, T]),
                                ALU.add).then_inc(s["z_ready"], 1)

            def b_copy(b, j):
                dve.wait_ge(s["bc_psum"], NBC * b + j + 1)
                v.tensor_copy(bc_sb[b][:, j * 512:(j + 1) * 512], work[:, j, :]).then_inc(s["bcB_ready"], 1)

            def softplus(b):
                dve.wait_ge(s["e_ready"], b + 1)
                v.tensor_scalar(cg[:, :, :], thg[:, :, :], 1.0, None, ALU.add).then_inc(s["w_ready"], 1)
                dve.wait_ge(s["w_ready"], b + 1)
                v.scalar_tensor_tensor(out=thg[:, :, :], in0=cg[:, :, :], scalar=-1.0, in1=thg[:, :, :],
                                       op0=ALU.add, op1=ALU.subtract).then_inc(s["nc_ready"], 1)
                dve.wait_ge(s["nc_ready"], b + 1)
                v.scalar_tensor_tensor(out=z_sb[:, :, :], in0=z_sb[:, :, :], scalar=0.0, in1=thg[:, :, :],
                                       op0=ALU.max, op1=ALU.subtract).then_inc(s["q_ready"], 1)
                dve.wait_ge(s["q_ready"], b + 1)
                dve.wait_ge(s["ln_ready"], b + 1)
                v.tensor_tensor(dt_sb[:, b], z_sb[:, :, :], th[:, :, :], ALU.add).then_inc(s["dt_ready"], 1)
                dve.wait_ge(s["dt_ready"], b + 1)
                v.tensor_tensor(dtu_sb[:, b], dt_sb[:, b], u_sb[:, b], ALU.mult).then_inc(s["dtu_ready"], 1)

            def scan(b, i):
                k = CT * b + i
                cm = bc_sb[b][:, N * T:2 * N * T]
                flat = st[:, k % 2].rearrange("p n t -> p (n t)")
                dve.wait_ge(s["dA_ready"], k + 1)
                dve.wait_ge(s["dBu_ready"], k + 1)
                v.tensor_tensor_scan(flat, dA[:, k % 2].rearrange("p n t -> p (n t)"), flat, 0.0,
                                     ALU.mult, ALU.add).then_inc(s["scan_done"], 1)
                dve.wait_ge(s["scan_done"], k + 1)
                if i == 0:
                    dve.wait_ge(s["bcC_ready"], NBC // 2 * (b + 1))
                v.tensor_tensor(flat, flat, cm, ALU.mult).then_inc(s["mulC_done"], 1)
                dve.wait_ge(s["mulC_done"], k + 1)
                if k:
                    dve.wait_ge(s["y2_ready"], k)
                v.reduce_sum(y_sb[:, :], st[:, k % 2].rearrange("p n t -> p t n"), AX.X).then_inc(s["y_ready"], 1)
                dve.wait_ge(s["y_ready"], k + 1)
                if k:
                    dve.wait_ge(s["yg_ready"], k)
                v.scalar_tensor_tensor(out=y2_sb[:, :], in0=u_sb[:, b, i], scalar=chan_sb[:, i, TAPS + 2:TAPS + 3],
                                       in1=y_sb[:, :], op0=ALU.mult, op1=ALU.add).then_inc(s["y2_ready"], 1)
                dve.wait_ge(s["y2_ready"], k + 1)
                v.scalar_tensor_tensor(out=sg_sb[:, b, i], in0=y2_sb[:, :], scalar=0.5, in1=sg_sb[:, b, i],
                                       op0=ALU.mult, op1=ALU.mult).then_inc(s["yg_ready"], 1)

            def residual2(b):
                dve.wait_ge(s["op_ready"], b + 1)
                v.tensor_tensor(x2_sb[:, b, :], op_ps, x1_sb[:, b, :], ALU.add).then_inc(s["x2_ready"], 1)
                dve.wait_ge(s["x2_ready"], b + 1)
                ln_stats(2, b, x2_sb[:, b, :])
                ln_apply(2, b, x2_sb[:, b, :])

            def route(b):
                dve.wait_ge(s["lg_ready"], b + 1)
                v.tensor_reduce(nlg[:, b:b + 1], lg_ps, AX.X, ALU.max, negate=True).then_inc(s["nlg_ready"], 1)
                dve.wait_ge(s["ex_ready"], b + 1)
                v.reciprocal(exr[:, :], exs[:, :]).then_inc(s["exr_ready"], 1)
                dve.wait_ge(s["exr_ready"], b + 1)
                v.tensor_scalar(sc[:, 0:E], ex[:, :], exr[:, 0:1], None, ALU.mult).then_inc(s["sc_ready"], 1)
                dve.wait_ge(s["sc_ready"], b + 1)
                v.max(v8[:, :], sc[:, :]).then_inc(s["v8_ready"], 1)
                dve.wait_ge(s["v8_ready"], b + 1)
                v.reduce_sum(tks[:, :], v8[:, 0:TOPK], AX.X).then_inc(s["tks_ready"], 1)
                v.tensor_copy(v8[:, TOPK:8], sc[:, E:E + 2]).then_inc(s["v8s_ready"], 1)
                dve.wait_ge(s["v8s_ready"], b + 1)
                v.match_replace(out=rep[:, :], in_to_replace=v8[:, :], in_values=sc[:, :],
                                imm_value=0.0).then_inc(s["rep_ready"], 1)
                dve.wait_ge(s["tks_ready"], b + 1)
                v.tensor_scalar(tke[:, :], tks[:, :], 1e-20, None, ALU.add).then_inc(s["tke_ready"], 1)
                dve.wait_ge(s["tke_ready"], b + 1)
                v.reciprocal(tkr[:, :], tke[:, :]).then_inc(s["tkr_ready"], 1)
                dve.wait_ge(s["rep_ready"], b + 1)
                v.tensor_tensor(chosen[:, :], sc[:, 0:E], rep[:, 0:E], ALU.subtract).then_inc(s["chosen_ready"], 1)
                dve.wait_ge(s["chosen_ready"], b + 1)
                dve.wait_ge(s["tkr_ready"], b + 1)
                v.tensor_scalar(cw[:, b, 0:E], chosen[:, :], tkr[:, 0:1], 0.5, ALU.mult, ALU.mult)\
                    .then_inc(s["cw_ready"], 1)

            def ffn_h(b, p):
                if p == 0:
                    dve.wait_ge(s["cw_ready"], b + 1)
                k0 = 2 * (PAIRS * b + p)
                for k in (k0, k0 + 1):
                    dve.wait_ge(s["tg_ready"], k + 1)
                    v.scalar_tensor_tensor(out=tg[:, k % 4, :], in0=tg[:, k % 4, :], scalar=1.0,
                                           in1=work[:, k % 4, 0:I], op0=ALU.add, op1=ALU.mult)\
                        .then_inc(s["t1_ready"], 1)
                if k0 >= 4:
                    dve.wait_ge(s["tr_ready"], k0 // 2 - 1)
                for k in (k0, k0 + 1):
                    e = k - k0
                    dve.wait_ge(s["t1_ready"], k + 1)
                    v.scalar_tensor_tensor(out=h_sb[:, (k0 // 2) % 2, e * I:(e + 1) * I], in0=tg[:, k % 4, :],
                                           scalar=cw[:, b, 2 * p + e:2 * p + e + 1],
                                           in1=work[:, k % 4, I:2 * I], op0=ALU.mult, op1=ALU.mult)\
                        .then_inc(s["hf_ready"], 1)

            def finish(b):
                dve.wait_ge(s["w2_done"], PAIRS * (b + 1))
                v.tensor_tensor(fin_sb[:, b, :], acc_ps[:, b * D:(b + 1) * D], x2_sb[:, b, :],
                                ALU.add).then_inc(s["fin_ready"], 1)

            v.memset(ones_bf[:, :], 1.0).then_inc(s["ones_ready"], 1)
            v.memset(hpad[:, :, 0:TAPS - 1], 0.0).then_inc(s["pads_ready"], 1)
            for k in range(2):
                v.memset(dA[:, k, :, 0:1], 0.0).then_inc(s["dA0_ready"], 1)
            v.memset(cw[:, :, E:E + 2], 0.5).then_inc(s["cw_const"], 1)
            v.memset(sc[:, E:E + 1], -1.0).then_inc(s["sentinel"], 1)
            v.memset(sc[:, E + 1:E + 2], -2.0).then_inc(s["sentinel"], 1)
            dve.wait_ge(ld_x, 16)
            ln_stats(0, 0, x_sb[:, 0, :])
            ln_stats(0, 1, x_sb[:, 1, :])
            ln_apply(0, 0, x_sb[:, 0, :])
            ln_apply(0, 1, x_sb[:, 1, :])
            dve.wait_ge(ld_mask, 16)
            v.tensor_scalar(mask_sb[:, :], mask_u8[:, :], 1.0, -MASKED, ALU.subtract, ALU.mult)\
                .then_inc(s["mask_ready"], 1)
            dve.wait_ge(s["ident_ready"], 1)
            v.tensor_copy(ident_bf[:, :], ident[:, :]).then_inc(s["ident_bf_ready"], 1)
            Q = 2 * N
            v.tensor_tensor(tmp_pick[:, :], ident[0:3 * Q, 0:Q], ident[0:3 * Q, Q:2 * Q],
                            ALU.add).then_inc(s["pick_half"], 1)
            dve.wait_ge(s["pick_half"], 1)
            v.tensor_tensor(pick[:, :], tmp_pick[:, :], ident[0:3 * Q, 2 * Q:3 * Q],
                            ALU.add).then_inc(s["pick_ready"], 1)
            score_max(0)
            pT_copy(0, 1)
            pT_copy(0, 3)
            attn_sums(0)
            dve.wait_ge(ld_chan, 16)
            v.tensor_scalar(half_sb[:, :, :], chan_sb[:, :, 0:TAPS + 1], 0.5, None, ALU.mult)\
                .then_inc(s["half_ready"], 1)
            dve.wait_ge(s["A_exp"], 1)
            v.tensor_scalar(negA_sb[:, :, :], negA_sb[:, :, :], -1.0, None, ALU.mult).then_inc(s["A_ready"], 1)
            residual1(0)
            dve.wait_ge(s["half_ready"], 1)
            dve.wait_ge(s["pads_ready"], 1)
            conv(0)
            normed(0)
            partsT_copy(0)
            dt_bias(0)
            for j in range(4):
                b_copy(0, j)
            softplus(0)
            scan(0, 0)
            score_max(1)
            scan(0, 1)
            pT_copy(1, 1)
            pT_copy(1, 3)
            attn_sums(1)
            residual1(1)
            conv(1)
            normed(1)
            partsT_copy(1)
            scan(0, 2)
            dt_bias(1)
            for j in range(4):
                b_copy(1, j)
            softplus(1)
            scan(0, 3)
            residual2(0)
            dve.wait_ge(s["sentinel"], 2)
            dve.wait_ge(s["cw_const"], 1)
            route(0)
            for i in range(CT):
                scan(1, i)
                ffn_h(0, 2 * i)
                ffn_h(0, 2 * i + 1)
            for p in range(2 * CT, PAIRS):
                ffn_h(0, p)
            residual2(1)
            finish(0)
            route(1)
            for p in range(PAIRS):
                ffn_h(1, p)
            finish(1)

        @block.tensor
        def _(pe):
            t_ = nc.tensor

            def xT(l, b):
                pe.wait_ge(xn_ready[l], b + 1)
                if l == 0 and b == 0:
                    pe.wait_ge(s["ident_ready"], 1)
                for c in range(KD):
                    last = t_.transpose(xt_ps[:, c * P:(c + 1) * P], xn_sb[:, b, c * P:(c + 1) * P], ident[:, :])
                last.then_inc(xT_psum[l], 1)

            def attention(b):
                xT(0, b)
                pe.wait_ge(xT_ready[0], b + 1)
                pe.wait_ge(s["mask_ready"], 1)
                pe.wait_ge(s["ones_ready"], 1)
                if b:
                    pe.wait_ge(s["bcC_ready"], NBC // 2 * b)
                for j in range(KB):
                    pe.wait_ge(ld_ctxT[b][j], 16)
                    for c in range(KD):
                        t_.matmul(work[:, j, :], xT_sb[:, b, c, :], ctxT_sb(b)[:, c, j * 512:(j + 1) * 512],
                                  start=(c == 0), stop=False)
                    lo = b * KEYS + j * 512
                    t_.matmul(work[:, j, :], ones_bf[:, :], mask_sb[:, lo:lo + 512],
                              start=False, stop=True).then_inc(s["scores_ready"], 1)
                for j in range(KB):
                    pe.wait_ge(s["probs_ready"], KB * b + j + 1)
                    for c in range(4):
                        lo = j * 512 + c * P
                        last = t_.transpose(work[:, j, c * P:(c + 1) * P], p_sb[:, lo:lo + P], ident[:, :])
                    last.then_inc(s["pT_psum"], 1)
                for j in range(KB):
                    pe.wait_ge(s["pT_dve" if j % 2 else "pT_act"], KB // 2 * b + j // 2 + 1)
                    pe.wait_ge(ld_ctxN[b][j // 2], 16)
                    for c in range(4 * j, 4 * j + 4):
                        last = t_.matmul(ro_ps, pT_sb[:, c, :], ctxN_sb(b)[:, c, :],
                                         start=(c == 0), stop=(c == 4 * KB - 1))
                last.then_inc(s["readout_ready"], 1)

            def front(b):
                xT(1, b)
                pe.wait_ge(xT_ready[1], b + 1)
                pe.wait_ge(ld_inw, 16)
                for half, ready in ((0, "h_ready"), (1, "gate_ready")):
                    for i in range(CT):
                        for c in range(KD):
                            lo = half * C + i * P
                            last = t_.matmul(work[:, half, i * T:(i + 1) * T], inw_sb[:, c, lo:lo + P],
                                             xT_sb[:, b, c, :], start=(c == 0), stop=(c == KD - 1))
                    last.then_inc(s[ready], 1)
                pe.wait_ge(s["u_ready"], b + 1)
                pe.wait_ge(ld_xw, 16)
                for i in range(CT):
                    last = t_.matmul(work[:, 2, 0:R + 2 * N], u_sb[:, b, i, :], xw_sb[:, i, :],
                                     start=(i == 0), stop=(i == CT - 1))
                last.then_inc(s["xp_ready"], 1)
                pe.wait_ge(s["dtn_ready"], b + 1)
                pe.wait_ge(s["bcn_ready"], b + 1)
                t_.transpose(work[:, 2, 256:256 + T], dtn[:, :], ident[:, :]).then_inc(s["dtT_psum"], 1)
                pe.wait_ge(s["part2"], b + 1)
                pe.wait_ge(s["ident_bf_ready"], 1)
                t_.transpose(tr_ps[0:6 * N, 0:T // 2].bitcast(BF16), parts[:, :, :, :].rearrange("p a b n -> p (a b n)"),
                             ident_bf[:, :]).then_inc(s["partsT_psum"], 1)
                pe.wait_ge(s["dtT_ready"], b + 1)
                pe.wait_ge(ld_dtw, 16)
                for i in range(CT):
                    last = t_.matmul(work[:, 3, i * T:(i + 1) * T], dtw_sb[:, i * P:(i + 1) * P], dtT[:, :],
                                     start=True, stop=True)
                last.then_inc(s["z_psum"], 1)
                pe.wait_ge(s["partsT_ready"], b + 1)
                pe.wait_ge(s["pick_ready"], 1)
                pe.wait_ge(s["sg_ready"], b + 1)
                for j in range(NBC):
                    if j == 3:
                        pe.wait_ge(s["z_ready"], b + 1)
                    if j >= 4:
                        pe.wait_ge(s["bcB_ready"], NBC // 2 * b + j - 3)
                    for q in range(4):
                        n = 4 * j + q
                        last = t_.matmul(work[:, j % 4, q * T:(q + 1) * T],
                                         pick[:, n:n + 1].to_broadcast([3 * 2 * N, P]), partsT[:, :],
                                         start=True, stop=True)
                    last.then_inc(s["bc_psum"], 1)

            def out_proj(b):
                pe.wait_ge(s["yg_ready"], CT * (b + 1))
                pe.wait_ge(s["x1_ready"], B)
                pe.wait_ge(ld_outw, 16)
                for i in range(CT):
                    last = t_.matmul(op_ps, sg_sb[:, b, i, :], outw_sb[:, i, :], start=(i == 0), stop=(i == CT - 1))
                last.then_inc(s["op_ready"], 1)

            def router(b):
                xT(2, b)
                pe.wait_ge(xT_ready[2], b + 1)
                pe.wait_ge(ld_gw, 16)
                for c in range(KD):
                    last = t_.matmul(lg_ps, xT_sb[:, b, c, :], gw_sb[:, c, :], start=(c == 0), stop=(c == KD - 1))
                last.then_inc(s["lg_ready"], 1)

            def gate_up(b, p):
                pe.wait_ge(ld_w13[p], 16)
                for e in range(2):
                    k = 2 * (PAIRS * b + p) + e
                    if k >= 4:
                        pe.wait_ge(s["hf_ready"], k - 3)
                    else:
                        pe.wait_ge(s["bcC_ready"], NBC // 2 * B)
                    for c in range(KD):
                        last = t_.matmul(work[:, k % 4, 0:2 * I], xT_sb[:, b, c, :], w13_sb(p)[:, c, e, :],
                                         start=(c == 0), stop=(c == KD - 1))
                    last.then_inc(s["gu_ready"], 1)

            def down(b, p):
                k = PAIRS * b + p
                pe.wait_ge(s["hf_ready"], 2 * k + 2)
                if k:
                    pe.wait_ge(s["hT_ready"], 2 * k)
                for c, (lo, m) in enumerate(HC):
                    last = t_.transpose(tr_ps[0:m, c * P:c * P + T], h_sb[:, k % 2, lo:lo + m], ident[:, :])
                last.then_inc(s["tr_ready"], 1)
                pe.wait_ge(s["hT_ready"], 2 * k + 2)
                pe.wait_ge(ld_w2[p], 32)
                if p == 0 and b:
                    pe.wait_ge(s["fin_ready"], b)
                for c, (lo, m) in enumerate(HC):
                    last = t_.matmul(acc_ps[:, b * D:(b + 1) * D], hT[0:m, k % 2, c * P:(c + 1) * P],
                                     w2_sb(p)[0:m, c, :], start=(p == 0 and c == 0),
                                     stop=(p == PAIRS - 1 and c == 2))
                last.then_inc(s["w2_done"], 1)

            attention(0)
            front(0)
            attention(1)
            front(1)
            out_proj(0)
            router(0)
            gate_up(0, 0)
            for p in range(1, PAIRS):
                gate_up(0, p)
                down(0, p - 1)
            down(0, PAIRS - 1)
            out_proj(1)
            router(1)
            gate_up(1, 0)
            for p in range(1, PAIRS):
                gate_up(1, p)
                down(1, p - 1)
            down(1, PAIRS - 1)


def kernel(**inputs):
    import numpy as np
    import concourse.bacc as bacc
    from concourse.bass_utils import run_bass_kernel_spmd as run

    a = {k: np.asarray(v) for k, v in inputs.items()}
    C = a["L0_attn_out_proj_w"].shape[0]
    chan = np.concatenate([a["L0_attn_conv_w"][:, 0, :], a["L0_attn_conv_b"][:, None],
                           a["L0_attn_dt_proj_b"][:, None], a["L0_attn_D_param"][:, None],
                           a["L0_attn_A_log"]], axis=1)
    chan = chan.reshape(C // 128, 128, -1).transpose(1, 0, 2)
    E, I2, D = a["L0_ffn_w13"].shape
    I = I2 // 2
    sw13 = a["L0_ffn_sw13"].reshape(2, 2, I, D).transpose(1, 0, 2, 3).reshape(2, I2, D)
    w13 = np.concatenate([a["L0_ffn_w13"], sw13], axis=0).reshape(-1, 2, I2, D).transpose(0, 3, 1, 2)
    w2 = np.concatenate([a["L0_ffn_w2"].transpose(0, 2, 1).reshape(-1, D), a["L0_ffn_sw2"].T], axis=0)
    arrays = {
        "x": a["x"], "ctx_t": a["ctx_2048"].transpose(0, 2, 1), "ctx_n": a["ctx_2048"],
        "mask": a["mask_BxS2_bk0"].reshape(1, -1), "in_w": a["L0_attn_in_proj_w"], "chan": chan,
        "x_w": a["L0_attn_x_proj_w"], "dt_w": a["L0_attn_dt_proj_w"], "out_w": a["L0_attn_out_proj_w"],
        "gate_w": a["L0_ffn_gate_w"].T, "w13": w13, "w2": w2,
    }
    arrays = {k: np.ascontiguousarray(v) for k, v in arrays.items()}
    nc = bacc.Bacc("TRN2", target_bir_lowering=False, num_devices=1)
    args = [nc.dram_tensor(f"in_{k}", v.shape, mybir.dt.from_np(v.dtype), kind="ExternalInput").ap()
            for k, v in arrays.items()]
    out = nc.dram_tensor("out_0", a["x"].shape, F32, kind="ExternalOutput").ap()
    build(nc, *args, out)
    r = run(nc, [{f"in_{k}": v for k, v in arrays.items()}], core_ids=[0])
    return r.results[0]["out_0"]
```

```python
from contextlib import ExitStack

import concourse.bass as bass
from concourse import mybir

F32 = mybir.dt.float32
BF16 = mybir.dt.bfloat16
U8 = mybir.dt.uint8
ALU = mybir.AluOpType
ACT = mybir.ActivationFunctionType
AX = mybir.AxisListType

def build(nc, x, ctx_t, ctx_n, mask, in_w, chan, x_w, dt_w, out_w, gate_w, w13, w2, out):
    P = 128
    B, T, D = x.shape
    KEYS = ctx_n.shape[1]
    KD = D // P
    KB = KEYS // 512
    C = out_w.shape[0]
    CT = C // P
    R = dt_w.shape[0]
    N = (x_w.shape[1] - R) // 2
    TAPS = 4
    E = gate_w.shape[1]
    PAIRS = w13.shape[0]
    I = w13.shape[3] // 2
    TOPK = 6
    HC = [(0, P), (P, P), (2 * P, 2 * I - 2 * P)]
    SCALE = float(D) ** -0.5
    LN_EPS, RMS_EPS = 1e-5, 1e-6
    MASKED = -1e30
    NBC = 2 * N * T // 512

    with ExitStack() as ctx:
        def sb(name, shape, dt=F32):
            return ctx.enter_context(nc.sbuf_tensor(name, shape, dt))

        def psum(name, shape, dt=F32):
            return ctx.enter_context(nc.psum_tensor(name, shape, dt))

        def sem(name):
            return ctx.enter_context(nc.semaphore(name))

        work = psum("work", [P, 4, 512])
        tr_ps = psum("tr_ps", [P, 512])
        xt_ps = psum("xt_ps", [P, 512])
        tok_ps = psum("tok_ps", [P, 512])
        acc_ps = psum("acc_ps", [P, 512])
        ro_ps = tok_ps[:, 0:D]
        op_ps = tok_ps[:, D:2 * D]
        lg_ps = xt_ps[:, 256:256 + E]
        xp_ps = xt_ps[:, D:D + R + 2 * N]
        h_ps = acc_ps
        z_ps = acc_ps
        gate_ps = tr_ps
        dtT_ps = tr_ps[:, 0:T]
        partsT_ps = tr_ps[0:6 * N, T:T + T // 2].bitcast(BF16)
        bc_ps = [tr_ps, acc_ps]

        w13_len = PAIRS * KD * 4 * I
        w2_len = PAIRS * 3 * D
        big = sb("big", [P, w13_len + w2_len])
        ctx_len = KD * KEYS

        def ctxT_sb(b):
            return big[:, 2 * b * ctx_len:(2 * b + 1) * ctx_len].rearrange("p (c k) -> p c k", c=KD)

        def ctxN_sb(b):
            return big[:, (2 * b + 1) * ctx_len:(2 * b + 2) * ctx_len].rearrange("p (c d) -> p c d", d=D)

        def w13_sb(p):
            n = KD * 4 * I
            return big[:, p * n:(p + 1) * n].rearrange("p (c e i) -> p c e i", c=KD, e=2)

        def w2_off(p):
            return w13_len + (PAIRS - 1 - p) * 3 * D

        def w2_sb(p):
            return big[:, w2_off(p):w2_off(p) + 3 * D].rearrange("p (c d) -> p c d", c=3)

        inw_sb = sb("inw_sb", [P, KD, 2 * C])
        xw_sb = sb("xw_sb", [P, CT, R + 2 * N])
        dtw_sb = sb("dtw_sb", [P, C])
        outw_sb = sb("outw_sb", [P, CT, D])
        gw_sb = sb("gw_sb", [P, KD, E])
        NCH = TAPS + 3 + N
        chan_sb = sb("chan_sb", [P, CT, NCH])
        half_sb = sb("half_sb", [P, CT, TAPS + 1])
        negA_sb = sb("negA_sb", [P, CT, N])
        ones_bf = sb("ones_bf", [1, P], BF16)
        ident = sb("ident", [P, P])
        ident_bf = sb("ident_bf", [P, P], BF16)
        pick = sb("pick", [3 * 2 * N, 2 * N], BF16)
        tmp_pick = sb("tmp_pick", [3 * 2 * N, 2 * N])
        neghalf = sb("neghalf", [P, 3])

        x_sb = sb("x_sb", [P, B, D])
        x1_sb = sb("x1_sb", [P, B, D])
        x2_sb = sb("x2_sb", [P, B, D])
        fin_sb = x1_sb
        stats = sb("stats", [P, B, 3, 6])
        mv = sb("mv", [P, B, 3, 2])
        ve = sb("ve", [P, B, 3])
        rstd = sb("rstd", [P, B, 3])
        xn_sb = sb("xn_sb", [P, B, D])
        xT_sb = sb("xT_sb", [P, B, KD, T])

        probs = sb("probs", [P, 2, KEYS])
        p_sb = probs[:, 0, :]
        pT_sb = probs[:, 1, :].rearrange("p (c t) -> p c t", t=T)
        bc0 = sb("bc0", [P, 2 * N * T])
        bc_sb = [bc0[:, :], probs[:, :, :].rearrange("p a k -> p (a k)")]
        mx4 = sb("mx4", [P, B, KB])
        mx = sb("mx", [P, B])
        nm = sb("nm", [P, B])
        valid = sb("valid", [P, B])
        sum4 = sb("sum4", [P, B, KB])
        rsum = sb("rsum", [P, B])
        rinv = sb("rinv", [P, B])
        rvalid = sb("rvalid", [P, B])

        hpad = sb("hpad", [P, CT, T + TAPS - 1])
        cg = sb("cg", [P, CT, T])
        th = sb("th", [P, CT, T])
        thg = sb("thg", [P, CT, T])
        z_sb = sb("z_sb", [P, CT, T])
        u_sb = sb("u_sb", [P, B, CT, T])
        sg_sb = sb("sg_sb", [P, B, CT, T])
        dt_sb = sb("dt_sb", [P, B, CT, T])
        dtu_sb = sb("dtu_sb", [P, B, CT, T])
        ss = sb("ss", [P, B, 3])
        sse = sb("sse", [P, B, 3])
        rr = sb("rr", [P, B, 3])
        dtn = sb("dtn", [P, R])
        dtT = sb("dtT", [P, T])
        bcn = sb("bcn", [P, 2, N])
        bcr = sb("bcr", [P, 2, N])
        parts = sb("parts", [P, 3, 2, N], BF16)
        partsT = sb("partsT", [3 * 2 * N, T], BF16)

        NH = N // 2
        dA = sb("dA", [P, 4, NH, T])
        st = sb("st", [P, 4, NH, T])
        mask_u8 = st[0:1, 0:2].rearrange("p k n t -> p (k n t)")[:, 0:B * KEYS // 4].bitcast(U8)
        y_sb = sb("y_sb", [P, T])
        y2_sb = sb("y2_sb", [P, T])

        ffn_buf = sb("ffn_buf", [P, 8 * I + 6 * P])
        tg = ffn_buf[:, 0:4 * I].rearrange("p (k i) -> p k i", k=4)
        h_sb = ffn_buf[:, 4 * I:8 * I].rearrange("p (k i) -> p k i", k=2)
        hT = ffn_buf[:, 8 * I:8 * I + 6 * P].rearrange("p (k c) -> p k c", k=2)
        mask_sb = ffn_buf[0:1, 0:B * KEYS // 2].bitcast(BF16)
        nlg = sb("nlg", [P, B])
        ex = sb("ex", [P, E])
        exs = sb("exs", [P, 1])
        exr = sb("exr", [P, 1])
        sc = sb("sc", [P, E + 2])
        rep = sb("rep", [P, E + 2])
        v8 = sb("v8", [P, 8])
        chosen = sb("chosen", [P, E])
        tks = sb("tks", [P, 1])
        tke = sb("tke", [P, 1])
        tkr = sb("tkr", [P, 1])
        cw = sb("cw", [P, B, E + 2])

        ld_x, ld_mask, ld_inw, ld_chan = sem("ld_x"), sem("ld_mask"), sem("ld_inw"), sem("ld_chan")
        ld_xw, ld_dtw, ld_outw, ld_gw = sem("ld_xw"), sem("ld_dtw"), sem("ld_outw"), sem("ld_gw")
        ld_ctxT = [[sem(f"ld_ctxT{b}{j}") for j in range(KB)] for b in range(B)]
        ld_ctxN = [[sem(f"ld_ctxN{b}{j}") for j in range(2)] for b in range(B)]
        ld_ffn = [sem(f"ld_ffn{p}") for p in range(PAIRS)]
        stored = sem("stored")
        s = {}
        for name in """zeroed ident_ready ident_bf_ready pick_half pick_ready mask_ready ones_ready consts_ready
                half_ready A_exp A_ready pads_ready dA0_ready
                scores_ready max4_done max_done nm_ready valid_ready probs_ready pT_psum pT_act pT_dve
                readout_ready sum_done rinv_done rvalid_ready x1_ready
                h_ready gate_ready hpad_ready tap0_done tap_done tanh_h u_ready tanh_g sg_ready
                xp_ready ss_ready sse_ready rr_ready dtn_ready bcn_ready part0 rest1 part1 part2
                dtT_psum dtT_ready partsT_psum partsT_ready z_psum z_ready abs_ready e_ready w_ready nc_ready
                ln_ready q_ready dt_ready dtu_ready bc_psum bc_even bc_odd y_psum folded
                dA_ready dBu_ready scan_done mulC_done y_ready y2_ready yg_ready
                op_ready x2_ready
                lg_ready nlg_ready ex_ready exr_ready sc_ready v8_ready v8s_ready tks_ready rep_ready chosen_ready
                tke_ready tkr_ready cw_ready cw_const sentinel
                gu_ready tg_ready t1_ready hf_ready tr_ready hT_ready w2_done fin_ready""".split():
            s[name] = sem(name)
        bn_done = [sem(f"bn_done{l}") for l in range(3)]
        var_ready = [sem(f"var_ready{l}") for l in range(3)]
        ve_ready = [sem(f"ve_ready{l}") for l in range(3)]
        rstd_ready = [sem(f"rstd_ready{l}") for l in range(3)]
        xn_ready = [sem(f"xn_ready{l}") for l in range(3)]
        xT_psum = [sem(f"xT_psum{l}") for l in range(3)]
        xT_ready = [sem(f"xT_ready{l}") for l in range(3)]

        def state_used(eng, m):
            k = m // 2
            if k < CT:
                eng.wait_ge(s["y_psum"], m + 1)
            elif m % 2:
                eng.wait_ge(s["folded"], k - CT + 1)
            else:
                eng.wait_ge(s["y_ready"], k - CT + 1)

        def bc_copied(eng, b, n):
            eng.wait_ge(s["bc_even"], NBC // 2 * b + (n + 1) // 2)
            if n > 1:
                eng.wait_ge(s["bc_odd"], NBC // 2 * b + n // 2)

        block = ctx.enter_context(nc.Block())

        @block.sync
        def _(sp):
            def load_ctx(b):
                src = ctx_t[b].rearrange("(c p) k -> p c k", p=P)
                for j in range(KB):
                    sp.dma_start(ctxT_sb(b)[:, :, j * 512:(j + 1) * 512],
                                 src[:, :, j * 512:(j + 1) * 512]).then_inc(ld_ctxT[b][j], 16)
                nat = ctx_n[b].rearrange("(c p) d -> p c d", p=P)
                half = KEYS // P // 2
                for j in range(2):
                    sp.dma_start(ctxN_sb(b)[:, j * half:(j + 1) * half, :],
                                 nat[:, j * half:(j + 1) * half, :]).then_inc(ld_ctxN[b][j], 16)

            sp.dma_start(x_sb[:, :, :], x.rearrange("b t d -> t b d")).then_inc(ld_x, 16)
            sp.dma_start(mask_u8[:, :], mask).then_inc(ld_mask, 16)
            load_ctx(0)
            sp.dma_start(inw_sb[:, :, :], in_w.rearrange("(c p) n -> p c n", p=P)).then_inc(ld_inw, 16)
            sp.dma_start(chan_sb[:, :, :], chan).then_inc(ld_chan, 16)
            sp.dma_start(xw_sb[:, :, :], x_w.rearrange("(c p) n -> p c n", p=P)).then_inc(ld_xw, 16)
            sp.dma_start(dtw_sb[:, :], dt_w).then_inc(ld_dtw, 16)
            load_ctx(1)
            sp.dma_start(outw_sb[:, :, :], out_w.rearrange("(c p) n -> p c n", p=P)).then_inc(ld_outw, 16)
            sp.dma_start(gw_sb[:, :, :], gate_w.rearrange("(c p) n -> p c n", p=P)).then_inc(ld_gw, 16)

            def load_w13(p):
                sp.dma_start(w13_sb(p), w13[p].rearrange("(c k) e i -> k c e i", k=P)).then_inc(ld_ffn[p], 16)

            def load_w2(p):
                rows = w2[p * 2 * I:(p + 1) * 2 * I, :]
                sp.dma_start(w2_sb(p)[:, 0:2, :],
                             rows[0:2 * P, :].rearrange("(c k) d -> k c d", k=P)).then_inc(ld_ffn[p], 16)
                sp.dma_start(w2_sb(p)[0:HC[2][1], 2, :], rows[2 * P:2 * I, :]).then_inc(ld_ffn[p], 16)

            sp.wait_ge(s["readout_ready"], 1)
            n13 = KD * 4 * I
            early = [p for p in range(PAIRS) if (p + 1) * n13 <= 2 * ctx_len]
            early2 = [p for p in range(PAIRS) if w2_off(p) >= 4 * ctx_len]
            for p in early:
                load_w13(p)
                if p in early2:
                    load_w2(p)
            sp.wait_ge(s["readout_ready"], 2)
            for p in range(PAIRS):
                if p not in early:
                    load_w13(p)
                if p not in early2 or p not in early:
                    load_w2(p)
            for b in range(B):
                sp.wait_ge(s["fin_ready"], b + 1)
                sp.dma_start(out[b], fin_sb[:, b, :]).then_inc(stored, 16)
            sp.wait_ge(stored, 16 * B)

        @block.gpsimd
        def _(pool):
            g = nc.gpsimd
            g.memset(ident[:, :], 0.0).then_inc(s["zeroed"], 1)
            pool.wait_ge(s["zeroed"], 1)
            g.affine_select(out=ident[:, :], in_=ident[:, :], compare_op=ALU.not_equal, fill=1.0, base=0,
                            pattern=[[-1, P]], channel_multiplier=1).then_inc(s["ident_ready"], 1)
            g.memset(neghalf[:, :], -0.5).then_inc(s["consts_ready"], 1)
            pool.wait_ge(s["consts_ready"], 1)

            def rsqrt_var(l, b):
                pool.wait_ge(var_ready[l], b + 1)
                g.tensor_scalar(ve[:, b, l:l + 1], mv[:, b, l, 1:2], LN_EPS, None, ALU.add).then_inc(ve_ready[l], 1)
                pool.wait_ge(ve_ready[l], b + 1)
                g.tensor_tensor(rstd[:, b, l:l + 1], ve[:, b, l:l + 1], neghalf[:, 0:1],
                                ALU.pow).then_inc(rstd_ready[l], 1)

            def rsqrt_rms(b):
                pool.wait_ge(s["ss_ready"], 3 * (b + 1))
                g.tensor_scalar(sse[:, b, :], ss[:, b, :], RMS_EPS, None, ALU.add).then_inc(s["sse_ready"], 1)
                pool.wait_ge(s["sse_ready"], b + 1)
                g.tensor_tensor(rr[:, b, :], sse[:, b, :], neghalf[:, :], ALU.pow).then_inc(s["rr_ready"], 1)

            def inputs(b, i, half):
                if i == 0 and half == 0:
                    pool.wait_ge(s["dtu_ready"], b + 1)
                    bc_copied(pool, b, NBC // 2)
                m = 2 * (CT * b + i) + half
                if m >= 4:
                    state_used(pool, m - 4)
                bm = bc_sb[b][:, half * NH * T:(half + 1) * NH * T].rearrange("p (n t) -> p n t", n=NH)
                g.tensor_tensor(st[:, m % 4], bm, dtu_sb[:, b, i:i + 1, :].to_broadcast([P, NH, T]),
                                ALU.mult).then_inc(s["dBu_ready"], 1)

            def fold(i):
                m = 2 * (CT + i)
                pool.wait_ge(s["mulC_done"], m + 2)
                g.tensor_tensor(st[:, m % 4], st[:, m % 4], st[:, (m + 1) % 4], ALU.add).then_inc(s["folded"], 1)

            rsqrt_var(0, 0)
            rsqrt_var(0, 1)
            rsqrt_var(1, 0)
            rsqrt_rms(0)
            inputs(0, 0, 0)
            inputs(0, 0, 1)
            rsqrt_var(1, 1)
            inputs(0, 1, 0)
            inputs(0, 1, 1)
            rsqrt_rms(1)
            for m in range(4, 8):
                inputs(0, m // 2, m % 2)
            inputs(1, 0, 0)
            inputs(1, 0, 1)
            rsqrt_var(2, 0)
            for i in range(1, CT):
                inputs(1, i, 0)
                inputs(1, i, 1)
                fold(i - 1)
            fold(CT - 1)
            rsqrt_var(2, 1)

        @block.scalar
        def _(act):
            a = nc.scalar

            def xT_copy(l, b):
                act.wait_ge(xT_psum[l], b + 1)
                a.copy(xT_sb[:, b].rearrange("p c t -> p (c t)"), xt_ps[:, 0:D]).then_inc(xT_ready[l], 1)

            def softmax_exp(b):
                act.wait_ge(s["nm_ready"], b + 1)
                for j in range(KB):
                    a.activation(p_sb[:, j * 512:(j + 1) * 512], work[:, j, :], ACT.Exp, bias=nm[:, b:b + 1],
                                 scale=SCALE, accum_out=sum4[:, b, j:j + 1]).then_inc(s["probs_ready"], 1)

            def pT_copy(b, j):
                act.wait_ge(s["pT_psum"], KB * b + j + 1)
                a.copy(probs[:, 1, j * 512:(j + 1) * 512], work[:, j, :]).then_inc(s["pT_act"], 1)

            def gate_tanh(b):
                if b:
                    act.wait_ge(s["dt_ready"], b)
                act.wait_ge(s["gate_ready"], b + 1)
                a.activation(thg[:, :, :].rearrange("p c t -> p (c t)"), gate_ps[:, :], ACT.Tanh,
                             scale=0.5).then_inc(s["tanh_g"], 1)

            def conv_tanh(b):
                act.wait_ge(s["tap_done"], (TAPS - 1) * CT * (b + 1))
                a.activation(th[:, :, :], cg[:, :, :], ACT.Tanh).then_inc(s["tanh_h"], 1)

            def squares(b):
                act.wait_ge(s["xp_ready"], b + 1)
                for k, (lo, n) in enumerate([(0, R), (R, N), (R + N, N)]):
                    a.activation(z_sb[:, k, 0:n], xp_ps[:, lo:lo + n], ACT.Square, scale=float(n) ** -0.5,
                                 accum_out=ss[:, b, k:k + 1]).then_inc(s["ss_ready"], 1)

            def dt_side(b):
                act.wait_ge(s["dtT_psum"], b + 1)
                a.copy(dtT[:, :], dtT_ps).then_inc(s["dtT_ready"], 1)

            def softplus_exp(b):
                act.wait_ge(s["z_ready"], b + 1)
                a.activation(th[:, :, :], z_sb[:, :, :], ACT.Abs).then_inc(s["abs_ready"], 1)
                act.wait_ge(s["abs_ready"], b + 1)
                a.activation(thg[:, :, :], th[:, :, :], ACT.Exp, scale=-1.0).then_inc(s["e_ready"], 1)

            def softplus_ln(b):
                act.wait_ge(s["w_ready"], b + 1)
                a.activation(th[:, :, :], cg[:, :, :], ACT.Ln).then_inc(s["ln_ready"], 1)

            def bc_copy(b, j):
                act.wait_ge(s["bc_psum"], NBC * b + j + 1)
                a.copy(bc_sb[b][:, j * 512:(j + 1) * 512], bc_ps[j % 2][:, :])\
                    .then_inc(s["bc_odd" if j % 2 else "bc_even"], 1)

            def decays(b, i, half):
                m = 2 * (CT * b + i) + half
                if m % (2 * CT) == 0:
                    act.wait_ge(s["dt_ready"], b + 1)
                if m >= 4:
                    act.wait_ge(s["scan_done"], m - 3)
                for n in range(NH):
                    nn = half * NH + n
                    last = a.activation(dA[:, m % 4, n, 1:T], dt_sb[:, b, i, 1:T], ACT.Exp,
                                        scale=negA_sb[:, i, nn:nn + 1])
                last.then_inc(s["dA_ready"], 1)

            def gate_exp(b):
                act.wait_ge(s["nlg_ready"], b + 1)
                a.activation(ex[:, :], lg_ps, ACT.Exp, bias=nlg[:, b:b + 1],
                             accum_out=exs[:, :]).then_inc(s["ex_ready"], 1)

            def ffn_tanh(b, p):
                for e in range(2):
                    k = 2 * (PAIRS * b + p) + e
                    act.wait_ge(s["gu_ready"], k + 1)
                    if k >= 4:
                        act.wait_ge(s["hf_ready"], k - 3)
                    a.activation(tg[:, k % 4, :], work[:, k % 4, 0:I], ACT.Tanh, scale=0.5).then_inc(s["tg_ready"], 1)

            def hT_copy(b, p):
                k = PAIRS * b + p
                act.wait_ge(s["tr_ready"], k + 1)
                if k >= 2:
                    act.wait_ge(s["w2_done"], k - 1)
                a.copy(hT[:, k % 2, 0:2 * P], tr_ps[:, 0:2 * P]).then_inc(s["hT_ready"], 1)
                m = HC[2][1]
                a.copy(hT[0:m, k % 2, 2 * P:3 * P], tr_ps[0:m, 2 * P:3 * P]).then_inc(s["hT_ready"], 1)

            xT_copy(0, 0)
            xT_copy(0, 1)
            softmax_exp(0)
            pT_copy(0, 0)
            pT_copy(0, 2)
            act.wait_ge(ld_chan, 16)
            a.activation(negA_sb[:, :, :], chan_sb[:, :, TAPS + 3:NCH], ACT.Exp).then_inc(s["A_exp"], 1)
            xT_copy(1, 0)
            gate_tanh(0)
            conv_tanh(0)
            softmax_exp(1)
            pT_copy(1, 0)
            pT_copy(1, 2)
            squares(0)

            dt_side(0)
            softplus_exp(0)
            softplus_ln(0)
            bc_copy(0, 1)
            bc_copy(0, 3)
            act.wait_ge(s["A_ready"], 1)
            act.wait_ge(s["dA0_ready"], 4)
            decays(0, 0, 0)
            bc_copy(0, 5)
            bc_copy(0, 7)
            decays(0, 0, 1)
            xT_copy(1, 1)
            decays(0, 1, 0)
            gate_tanh(1)
            decays(0, 1, 1)
            conv_tanh(1)
            squares(1)
            decays(0, 2, 0)
            dt_side(1)

            decays(0, 2, 1)
            softplus_exp(1)
            softplus_ln(1)
            decays(0, 3, 0)
            for j in range(4):
                bc_copy(1, j)
            decays(0, 3, 1)
            for j in range(4, NBC):
                bc_copy(1, j)
            decays(1, 0, 0)
            decays(1, 0, 1)
            xT_copy(2, 0)
            gate_exp(0)
            decays(1, 1, 0)
            ffn_tanh(0, 0)
            for p in range(1, PAIRS):
                ffn_tanh(0, p)
                hT_copy(0, p - 1)
                if p <= 5:
                    decays(1, (p + 2) // 2, p % 2)
            hT_copy(0, PAIRS - 1)
            xT_copy(2, 1)
            gate_exp(1)
            ffn_tanh(1, 0)
            for p in range(1, PAIRS):
                ffn_tanh(1, p)
                hT_copy(1, p - 1)
            hT_copy(1, PAIRS - 1)

        @block.vector
        def _(dve):
            v = nc.vector

            def ln_stats(l, b, src):
                v.bn_stats(stats[:, b, l, :], src).then_inc(bn_done[l], 1)
                dve.wait_ge(bn_done[l], b + 1)
                v.bn_aggr(mv[:, b, l, :], stats[:, b, l, :]).then_inc(var_ready[l], 1)

            def ln_apply(l, b, src):
                if l:
                    dve.wait_ge(xT_psum[l - 1], b + 1)
                dve.wait_ge(rstd_ready[l], b + 1)
                v.tensor_scalar(xn_sb[:, b, :], src, mv[:, b, l, 0:1], rstd[:, b, l:l + 1],
                                ALU.subtract, ALU.mult).then_inc(xn_ready[l], 1)

            def bank_max(b, j):
                dve.wait_ge(s["scores_ready"], KB * b + j + 1)
                v.reduce_max(mx4[:, b, j:j + 1], work[:, j, :], AX.X).then_inc(s["max4_done"], 1)

            def row_max(b):
                dve.wait_ge(s["max4_done"], KB * (b + 1))
                v.reduce_max(mx[:, b:b + 1], mx4[:, b, :], AX.X).then_inc(s["max_done"], 1)
                dve.wait_ge(s["max_done"], b + 1)
                v.tensor_scalar(nm[:, b:b + 1], mx[:, b:b + 1], -SCALE, None, ALU.mult).then_inc(s["nm_ready"], 1)
                v.tensor_scalar(valid[:, b:b + 1], mx[:, b:b + 1], 0.1 * MASKED, None,
                                ALU.is_gt).then_inc(s["valid_ready"], 1)

            def pT_copy(b, j):
                dve.wait_ge(s["pT_psum"], KB * b + j + 1)
                v.tensor_copy(probs[:, 1, j * 512:(j + 1) * 512], work[:, j, :]).then_inc(s["pT_dve"], 1)

            def attn_sums(b):
                dve.wait_ge(s["probs_ready"], KB * (b + 1))
                v.reduce_sum(rsum[:, b:b + 1], sum4[:, b, :], AX.X).then_inc(s["sum_done"], 1)
                dve.wait_ge(s["sum_done"], b + 1)
                v.reciprocal(rinv[:, b:b + 1], rsum[:, b:b + 1]).then_inc(s["rinv_done"], 1)
                dve.wait_ge(s["rinv_done"], b + 1)
                dve.wait_ge(s["valid_ready"], b + 1)
                v.tensor_tensor(rvalid[:, b:b + 1], rinv[:, b:b + 1], valid[:, b:b + 1],
                                ALU.mult).then_inc(s["rvalid_ready"], 1)

            def residual1(b):
                dve.wait_ge(s["readout_ready"], b + 1)
                dve.wait_ge(s["rvalid_ready"], b + 1)
                v.scalar_tensor_tensor(out=x1_sb[:, b, :], in0=ro_ps, scalar=rvalid[:, b:b + 1],
                                       in1=x_sb[:, b, :], op0=ALU.mult, op1=ALU.add).then_inc(s["x1_ready"], 1)
                dve.wait_ge(s["x1_ready"], b + 1)
                ln_stats(1, b, x1_sb[:, b, :])
                ln_apply(1, b, x1_sb[:, b, :])

            def conv(b):
                dve.wait_ge(s["h_ready"], b + 1)
                v.tensor_copy(hpad[:, :, TAPS - 1:], h_ps[:, :].rearrange("p (c t) -> p c t", c=CT))\
                    .then_inc(s["hpad_ready"], 1)
                dve.wait_ge(s["hpad_ready"], b + 1)
                for i in range(CT):
                    v.tensor_scalar(cg[:, i, :], hpad[:, i, TAPS - 1:], half_sb[:, i, TAPS - 1:TAPS],
                                    half_sb[:, i, TAPS:TAPS + 1], ALU.mult, ALU.add).then_inc(s["tap0_done"], 1)
                for k in range(TAPS - 1):
                    for i in range(CT):
                        if k:
                            dve.wait_ge(s["tap_done"], CT * ((TAPS - 1) * b + k - 1) + i + 1)
                        else:
                            dve.wait_ge(s["tap0_done"], CT * b + i + 1)
                        v.scalar_tensor_tensor(out=cg[:, i, :], in0=hpad[:, i, k:k + T],
                                               scalar=half_sb[:, i, k:k + 1], in1=cg[:, i, :],
                                               op0=ALU.mult, op1=ALU.add).then_inc(s["tap_done"], 1)
                dve.wait_ge(s["tanh_g"], b + 1)
                v.scalar_tensor_tensor(out=sg_sb[:, b].rearrange("p c t -> p (c t)"),
                                       in0=thg[:, :, :].rearrange("p c t -> p (c t)"), scalar=1.0,
                                       in1=gate_ps[:, :], op0=ALU.add, op1=ALU.mult).then_inc(s["sg_ready"], 1)
                dve.wait_ge(s["tanh_h"], b + 1)
                v.scalar_tensor_tensor(out=u_sb[:, b], in0=th[:, :, :], scalar=1.0, in1=cg[:, :, :],
                                       op0=ALU.add, op1=ALU.mult).then_inc(s["u_ready"], 1)

            def normed(b):
                dve.wait_ge(s["rr_ready"], b + 1)
                v.tensor_scalar(dtn[:, :], xp_ps[:, 0:R], rr[:, b, 0:1], None, ALU.mult)\
                    .then_inc(s["dtn_ready"], 1)
                v.tensor_tensor(bcn[:, :, :], xp_ps[:, R:R + 2 * N].rearrange("p (a n) -> p a n", a=2),
                                rr[:, b, 1:3].unsqueeze(2).to_broadcast([P, 2, N]),
                                ALU.mult).then_inc(s["bcn_ready"], 1)
                dve.wait_ge(s["bcn_ready"], b + 1)
                v.tensor_copy(parts[:, 0], bcn[:, :, :]).then_inc(s["part0"], 1)
                dve.wait_ge(s["part0"], b + 1)
                v.tensor_tensor(bcr[:, :, :], bcn[:, :, :], parts[:, 0], ALU.subtract).then_inc(s["rest1"], 1)
                dve.wait_ge(s["rest1"], b + 1)
                v.tensor_copy(parts[:, 1], bcr[:, :, :]).then_inc(s["part1"], 1)
                dve.wait_ge(s["part1"], b + 1)
                v.tensor_tensor(parts[:, 2], bcr[:, :, :], parts[:, 1], ALU.subtract).then_inc(s["part2"], 1)

            def partsT_copy(b):
                dve.wait_ge(s["partsT_psum"], b + 1)
                v.tensor_copy(partsT[:, :], partsT_ps).then_inc(s["partsT_ready"], 1)

            def dt_bias(b):
                dve.wait_ge(s["z_psum"], b + 1)
                v.tensor_tensor(z_sb[:, :, :], z_ps[:, :].rearrange("p (c t) -> p c t", c=CT),
                                chan_sb[:, :, TAPS + 1:TAPS + 2].to_broadcast([P, CT, T]),
                                ALU.add).then_inc(s["z_ready"], 1)

            def bc_copy(b, j):
                dve.wait_ge(s["bc_psum"], NBC * b + j + 1)
                v.tensor_copy(bc_sb[b][:, j * 512:(j + 1) * 512], bc_ps[j % 2][:, :])\
                    .then_inc(s["bc_odd" if j % 2 else "bc_even"], 1)

            def softplus_w(b):
                dve.wait_ge(s["e_ready"], b + 1)
                v.tensor_scalar(cg[:, :, :], thg[:, :, :], 1.0, None, ALU.add).then_inc(s["w_ready"], 1)
                dve.wait_ge(s["w_ready"], b + 1)
                v.scalar_tensor_tensor(out=thg[:, :, :], in0=cg[:, :, :], scalar=-1.0, in1=thg[:, :, :],
                                       op0=ALU.add, op1=ALU.subtract).then_inc(s["nc_ready"], 1)

            def softplus_sum(b):
                dve.wait_ge(s["nc_ready"], b + 1)
                v.scalar_tensor_tensor(out=z_sb[:, :, :], in0=z_sb[:, :, :], scalar=0.0, in1=thg[:, :, :],
                                       op0=ALU.max, op1=ALU.subtract).then_inc(s["q_ready"], 1)
                dve.wait_ge(s["q_ready"], b + 1)
                dve.wait_ge(s["ln_ready"], b + 1)
                v.tensor_tensor(dt_sb[:, b], z_sb[:, :, :], th[:, :, :], ALU.add).then_inc(s["dt_ready"], 1)
                dve.wait_ge(s["dt_ready"], b + 1)
                v.tensor_tensor(dtu_sb[:, b], dt_sb[:, b], u_sb[:, b], ALU.mult).then_inc(s["dtu_ready"], 1)

            def scan(b, i, half):
                m = 2 * (CT * b + i) + half
                lo = (N + half * NH) * T
                flat = st[:, m % 4].rearrange("p n t -> p (n t)")
                dve.wait_ge(s["dA_ready"], m + 1)
                dve.wait_ge(s["dBu_ready"], m + 1)
                v.tensor_tensor_scan(flat, dA[:, m % 4].rearrange("p n t -> p (n t)"), flat, 0.0,
                                     ALU.mult, ALU.add).then_inc(s["scan_done"], 1)
                dve.wait_ge(s["scan_done"], m + 1)
                if i == 0 and half == 0:
                    bc_copied(dve, b, NBC)
                v.tensor_tensor(flat, flat, bc_sb[b][:, lo:lo + NH * T], ALU.mult).then_inc(s["mulC_done"], 1)

            def sum_folded(i):
                k = CT + i
                dve.wait_ge(s["folded"], i + 1)
                dve.wait_ge(s["y2_ready"], k)
                v.reduce_sum(y_sb[:, :], st[:, 2 * k % 4].rearrange("p n t -> p t n"), AX.X)\
                    .then_inc(s["y_ready"], 1)

            def gated(b, i):
                k = CT * b + i
                state_used(dve, 2 * k + 1 - b)
                if k:
                    dve.wait_ge(s["yg_ready"], k)
                v.scalar_tensor_tensor(out=y2_sb[:, :], in0=u_sb[:, b, i], scalar=chan_sb[:, i, TAPS + 2:TAPS + 3],
                                       in1=y_sb[:, :] if b else work[:, i, 0:T],
                                       op0=ALU.mult, op1=ALU.add).then_inc(s["y2_ready"], 1)
                dve.wait_ge(s["y2_ready"], k + 1)
                v.scalar_tensor_tensor(out=sg_sb[:, b, i], in0=y2_sb[:, :], scalar=0.5, in1=sg_sb[:, b, i],
                                       op0=ALU.mult, op1=ALU.mult).then_inc(s["yg_ready"], 1)

            def residual2(b):
                dve.wait_ge(s["op_ready"], b + 1)
                v.tensor_tensor(x2_sb[:, b, :], op_ps, x1_sb[:, b, :], ALU.add).then_inc(s["x2_ready"], 1)
                dve.wait_ge(s["x2_ready"], b + 1)
                ln_stats(2, b, x2_sb[:, b, :])
                ln_apply(2, b, x2_sb[:, b, :])

            def route(b):
                dve.wait_ge(s["lg_ready"], b + 1)
                v.tensor_reduce(nlg[:, b:b + 1], lg_ps, AX.X, ALU.max, negate=True).then_inc(s["nlg_ready"], 1)
                dve.wait_ge(s["ex_ready"], b + 1)
                v.reciprocal(exr[:, :], exs[:, :]).then_inc(s["exr_ready"], 1)
                dve.wait_ge(s["exr_ready"], b + 1)
                v.tensor_scalar(sc[:, 0:E], ex[:, :], exr[:, 0:1], None, ALU.mult).then_inc(s["sc_ready"], 1)
                dve.wait_ge(s["sc_ready"], b + 1)
                v.max(v8[:, :], sc[:, :]).then_inc(s["v8_ready"], 1)
                dve.wait_ge(s["v8_ready"], b + 1)
                v.reduce_sum(tks[:, :], v8[:, 0:TOPK], AX.X).then_inc(s["tks_ready"], 1)
                v.tensor_copy(v8[:, TOPK:8], sc[:, E:E + 2]).then_inc(s["v8s_ready"], 1)
                dve.wait_ge(s["v8s_ready"], b + 1)
                v.match_replace(out=rep[:, :], in_to_replace=v8[:, :], in_values=sc[:, :],
                                imm_value=0.0).then_inc(s["rep_ready"], 1)
                dve.wait_ge(s["tks_ready"], b + 1)
                v.tensor_scalar(tke[:, :], tks[:, :], 1e-20, None, ALU.add).then_inc(s["tke_ready"], 1)
                dve.wait_ge(s["tke_ready"], b + 1)
                v.reciprocal(tkr[:, :], tke[:, :]).then_inc(s["tkr_ready"], 1)
                dve.wait_ge(s["rep_ready"], b + 1)
                v.tensor_tensor(chosen[:, :], sc[:, 0:E], rep[:, 0:E], ALU.subtract).then_inc(s["chosen_ready"], 1)
                dve.wait_ge(s["chosen_ready"], b + 1)
                dve.wait_ge(s["tkr_ready"], b + 1)
                v.tensor_scalar(cw[:, b, 0:E], chosen[:, :], tkr[:, 0:1], 0.5, ALU.mult, ALU.mult)\
                    .then_inc(s["cw_ready"], 1)

            def ffn_h(b, p):
                if p == 0:
                    dve.wait_ge(s["cw_ready"], b + 1)
                k0 = 2 * (PAIRS * b + p)
                for k in (k0, k0 + 1):
                    dve.wait_ge(s["tg_ready"], k + 1)
                    v.scalar_tensor_tensor(out=tg[:, k % 4, :], in0=tg[:, k % 4, :], scalar=1.0,
                                           in1=work[:, k % 4, 0:I], op0=ALU.add, op1=ALU.mult)\
                        .then_inc(s["t1_ready"], 1)
                if k0 >= 4:
                    dve.wait_ge(s["tr_ready"], k0 // 2 - 1)
                for k in (k0, k0 + 1):
                    e = k - k0
                    dve.wait_ge(s["t1_ready"], k + 1)
                    v.scalar_tensor_tensor(out=h_sb[:, (k0 // 2) % 2, e * I:(e + 1) * I], in0=tg[:, k % 4, :],
                                           scalar=cw[:, b, 2 * p + e:2 * p + e + 1],
                                           in1=work[:, k % 4, I:2 * I], op0=ALU.mult, op1=ALU.mult)\
                        .then_inc(s["hf_ready"], 1)

            def finish(b):
                dve.wait_ge(s["w2_done"], PAIRS * (b + 1))
                v.tensor_tensor(fin_sb[:, b, :], acc_ps[:, b * D:(b + 1) * D], x2_sb[:, b, :],
                                ALU.add).then_inc(s["fin_ready"], 1)

            v.memset(ones_bf[:, :], 1.0).then_inc(s["ones_ready"], 1)
            v.memset(hpad[:, :, 0:TAPS - 1], 0.0).then_inc(s["pads_ready"], 1)
            for k in range(4):
                v.memset(dA[:, k, :, 0:1], 0.0).then_inc(s["dA0_ready"], 1)
            v.memset(cw[:, :, E:E + 2], 0.5).then_inc(s["cw_const"], 1)
            v.memset(sc[:, E:E + 1], -1.0).then_inc(s["sentinel"], 1)
            v.memset(sc[:, E + 1:E + 2], -2.0).then_inc(s["sentinel"], 1)
            dve.wait_ge(ld_x, 16)
            ln_stats(0, 0, x_sb[:, 0, :])
            ln_stats(0, 1, x_sb[:, 1, :])
            ln_apply(0, 0, x_sb[:, 0, :])
            ln_apply(0, 1, x_sb[:, 1, :])
            dve.wait_ge(ld_mask, 16)
            for b in range(B):
                v.tensor_scalar(mask_sb[:, b * KEYS:(b + 1) * KEYS], mask_u8[:, b * KEYS:(b + 1) * KEYS],
                                1.0, -MASKED, ALU.subtract, ALU.mult).then_inc(s["mask_ready"], 1)
            dve.wait_ge(s["ident_ready"], 1)
            v.tensor_copy(ident_bf[:, :], ident[:, :]).then_inc(s["ident_bf_ready"], 1)
            Q = 2 * N
            v.tensor_tensor(tmp_pick[:, :], ident[0:3 * Q, 0:Q], ident[0:3 * Q, Q:2 * Q],
                            ALU.add).then_inc(s["pick_half"], 1)
            dve.wait_ge(s["pick_half"], 1)
            v.tensor_tensor(pick[:, :], tmp_pick[:, :], ident[0:3 * Q, 2 * Q:3 * Q],
                            ALU.add).then_inc(s["pick_ready"], 1)
            for j in range(KB):
                bank_max(0, j)
            row_max(0)
            pT_copy(0, 1)
            pT_copy(0, 3)
            attn_sums(0)
            dve.wait_ge(ld_chan, 16)
            v.tensor_scalar(half_sb[:, :, :], chan_sb[:, :, 0:TAPS + 1], 0.5, None, ALU.mult)\
                .then_inc(s["half_ready"], 1)
            dve.wait_ge(s["A_exp"], 1)
            v.tensor_scalar(negA_sb[:, :, :], negA_sb[:, :, :], -1.0, None, ALU.mult).then_inc(s["A_ready"], 1)
            residual1(0)
            bank_max(1, 0)
            bank_max(1, 1)
            dve.wait_ge(s["half_ready"], 1)
            dve.wait_ge(s["pads_ready"], 1)
            conv(0)
            bank_max(1, 2)
            bank_max(1, 3)
            row_max(1)
            pT_copy(1, 1)
            pT_copy(1, 3)
            normed(0)
            partsT_copy(0)
            dt_bias(0)
            softplus_w(0)
            bc_copy(0, 0)
            softplus_sum(0)
            bc_copy(0, 2)
            attn_sums(1)
            bc_copy(0, 4)
            bc_copy(0, 6)
            scan(0, 0, 0)
            residual1(1)
            scan(0, 0, 1)
            conv(1)
            scan(0, 1, 0)
            gated(0, 0)
            normed(1)
            partsT_copy(1)
            scan(0, 1, 1)
            dt_bias(1)
            scan(0, 2, 0)
            gated(0, 1)
            softplus_w(1)
            softplus_sum(1)
            scan(0, 2, 1)
            scan(0, 3, 0)
            gated(0, 2)
            scan(0, 3, 1)
            gated(0, 3)
            residual2(0)
            scan(1, 0, 0)
            dve.wait_ge(s["sentinel"], 2)
            dve.wait_ge(s["cw_const"], 1)
            route(0)
            for p in range(2 * CT):
                ffn_h(0, p)
                if p < 2 * CT - 1:
                    scan(1, (p + 1) // 2, (p + 1) % 2)
                if p >= 2 and p % 2 == 0:
                    sum_folded(p // 2 - 1)
                    gated(1, p // 2 - 1)
            sum_folded(CT - 1)
            gated(1, CT - 1)
            for p in range(2 * CT, PAIRS):
                ffn_h(0, p)
            residual2(1)
            finish(0)
            route(1)
            for p in range(PAIRS):
                ffn_h(1, p)
            finish(1)

        @block.tensor
        def _(pe):
            t_ = nc.tensor

            def xT(l, b):
                pe.wait_ge(xn_ready[l], b + 1)
                if l == 0 and b == 0:
                    pe.wait_ge(s["ident_ready"], 1)
                for c in range(KD):
                    last = t_.transpose(xt_ps[:, c * P:(c + 1) * P], xn_sb[:, b, c * P:(c + 1) * P], ident[:, :])
                last.then_inc(xT_psum[l], 1)

            def scores(b, j):
                if j == 0:
                    pe.wait_ge(xT_ready[0], b + 1)
                if b:
                    pe.wait_ge(s["pT_dve" if j % 2 else "pT_act"], KB // 2 * (b - 1) + j // 2 + 1)
                pe.wait_ge(ld_ctxT[b][j], 16)
                for c in range(KD):
                    t_.matmul(work[:, j, :], xT_sb[:, b, c, :], ctxT_sb(b)[:, c, j * 512:(j + 1) * 512],
                              start=(c == 0), stop=False)
                if j == 0:
                    pe.wait_ge(s["mask_ready"], b + 1)
                    pe.wait_ge(s["ones_ready"], 1)
                lo = b * KEYS + j * 512
                t_.matmul(work[:, j, :], ones_bf[:, :], mask_sb[:, lo:lo + 512],
                          start=False, stop=True).then_inc(s["scores_ready"], 1)

            def transposes(b, j):
                pe.wait_ge(s["probs_ready"], KB * b + j + 1)
                for c in range(4):
                    lo = j * 512 + c * P
                    last = t_.transpose(work[:, j, c * P:(c + 1) * P], p_sb[:, lo:lo + P], ident[:, :])
                last.then_inc(s["pT_psum"], 1)

            def readout(b, c0, n):
                if c0 == 0 and b:
                    pe.wait_ge(s["x1_ready"], b)
                for c in range(c0, c0 + n):
                    j = c // 4
                    if c % 4 == 0:
                        pe.wait_ge(s["pT_dve" if j % 2 else "pT_act"], KB // 2 * b + j // 2 + 1)
                        pe.wait_ge(ld_ctxN[b][j // 2], 16)
                    last = t_.matmul(ro_ps, pT_sb[:, c, :], ctxN_sb(b)[:, c, :],
                                     start=(c == 0), stop=(c == 4 * KB - 1))
                if c0 + n == 4 * KB:
                    last.then_inc(s["readout_ready"], 1)

            def in_proj(b):
                xT(1, b)
                pe.wait_ge(xT_ready[1], b + 1)
                pe.wait_ge(ld_inw, 16)
                if b:
                    bc_copied(pe, b - 1, NBC)
                for half, dst, ready in ((0, h_ps, "h_ready"), (1, gate_ps, "gate_ready")):
                    for i in range(CT):
                        for c in range(KD):
                            lo = half * C + i * P
                            last = t_.matmul(dst[:, i * T:(i + 1) * T], inw_sb[:, c, lo:lo + P],
                                             xT_sb[:, b, c, :], start=(c == 0), stop=(c == KD - 1))
                    last.then_inc(s[ready], 1)

            def x_proj(b):
                if not b:
                    pe.wait_ge(xT_ready[0], B)
                pe.wait_ge(s["u_ready"], b + 1)
                pe.wait_ge(ld_xw, 16)
                for i in range(CT):
                    last = t_.matmul(xp_ps, u_sb[:, b, i, :], xw_sb[:, i, :], start=(i == 0), stop=(i == CT - 1))
                last.then_inc(s["xp_ready"], 1)

            def turn(b):
                pe.wait_ge(s["dtn_ready"], b + 1)
                pe.wait_ge(s["sg_ready"], b + 1)
                t_.transpose(dtT_ps, dtn[:, :], ident[:, :]).then_inc(s["dtT_psum"], 1)
                pe.wait_ge(s["part2"], b + 1)
                pe.wait_ge(s["ident_bf_ready"], 1)
                pe.wait_ge(s["dtT_ready"], b + 1)
                t_.transpose(partsT_ps, parts[:, :, :, :].rearrange("p a b n -> p (a b n)"),
                             ident_bf[:, :]).then_inc(s["partsT_psum"], 1)

            def dt_proj(b):
                pe.wait_ge(s["dtT_ready"], b + 1)
                pe.wait_ge(ld_dtw, 16)
                for i in range(CT):
                    last = t_.matmul(z_ps[:, i * T:(i + 1) * T], dtw_sb[:, i * P:(i + 1) * P], dtT[:, :],
                                     start=True, stop=True)
                last.then_inc(s["z_psum"], 1)

            def spread(b, j):
                if j == 0:
                    pe.wait_ge(s["partsT_ready"], b + 1)
                    pe.wait_ge(s["pick_ready"], 1)
                if j == 1:
                    pe.wait_ge(s["z_ready"], b + 1)
                if j >= 2:
                    pe.wait_ge(s["bc_odd" if j % 2 else "bc_even"], NBC // 2 * b + j // 2)
                for q in range(4):
                    n = 4 * j + q
                    last = t_.matmul(bc_ps[j % 2][:, q * T:(q + 1) * T],
                                     pick[:, n:n + 1].to_broadcast([3 * 2 * N, P]), partsT[:, :],
                                     start=True, stop=True)
                last.then_inc(s["bc_psum"], 1)

            def sum_states(m):
                pe.wait_ge(s["mulC_done"], m + 1)
                for n in range(NH):
                    last = t_.matmul(work[:, m // 2, 0:T], ident[:, :], st[:, m % 4, n, :],
                                     start=(m % 2 == 0 and n == 0), stop=(m % 2 == 1 and n == NH - 1))
                last.then_inc(s["y_psum"], 1)

            def out_proj(b):
                pe.wait_ge(s["yg_ready"], CT * (b + 1))
                pe.wait_ge(s["x1_ready"], B)
                pe.wait_ge(ld_outw, 16)
                for i in range(CT):
                    last = t_.matmul(op_ps, sg_sb[:, b, i, :], outw_sb[:, i, :], start=(i == 0), stop=(i == CT - 1))
                last.then_inc(s["op_ready"], 1)

            def router(b):
                xT(2, b)
                pe.wait_ge(xT_ready[2], b + 1)
                pe.wait_ge(ld_gw, 16)
                for c in range(KD):
                    last = t_.matmul(lg_ps, xT_sb[:, b, c, :], gw_sb[:, c, :], start=(c == 0), stop=(c == KD - 1))
                last.then_inc(s["lg_ready"], 1)

            def gate_up(b, p, *es):
                pe.wait_ge(ld_ffn[p], 48)
                for e in es or range(2):
                    k = 2 * (PAIRS * b + p) + e
                    if k >= 4:
                        pe.wait_ge(s["hf_ready"], k - 3)
                    else:
                        pe.wait_ge(s["yg_ready"], CT)
                    for c in range(KD):
                        last = t_.matmul(work[:, k % 4, 0:2 * I], xT_sb[:, b, c, :], w13_sb(p)[:, c, e, :],
                                         start=(c == 0), stop=(c == KD - 1))
                    last.then_inc(s["gu_ready"], 1)

            def turn_h(b, p):
                k = PAIRS * b + p
                pe.wait_ge(s["hf_ready"], 2 * k + 2)
                if k:
                    pe.wait_ge(s["hT_ready"], 2 * k)
                for c, (lo, m) in enumerate(HC):
                    last = t_.transpose(tr_ps[0:m, c * P:c * P + T], h_sb[:, k % 2, lo:lo + m], ident[:, :])
                last.then_inc(s["tr_ready"], 1)

            def down(b, p):
                k = PAIRS * b + p
                pe.wait_ge(s["hT_ready"], 2 * k + 2)
                pe.wait_ge(ld_ffn[p], 48)
                if p == 0 and b:
                    pe.wait_ge(s["fin_ready"], b)
                for c, (lo, m) in enumerate(HC):
                    last = t_.matmul(acc_ps[:, b * D:(b + 1) * D], hT[0:m, k % 2, c * P:(c + 1) * P],
                                     w2_sb(p)[0:m, c, :], start=(p == 0 and c == 0),
                                     stop=(p == PAIRS - 1 and c == 2))
                last.then_inc(s["w2_done"], 1)

            xT(0, 0)
            scores(0, 0)
            xT(0, 1)
            for j in range(1, KB):
                scores(0, j)
            for j in range(KB):
                transposes(0, j)
            readout(0, 0, 4 * KB)
            scores(1, 0)
            scores(1, 1)
            in_proj(0)
            scores(1, 2)
            scores(1, 3)
            x_proj(0)
            for j in range(KB):
                transposes(1, j)
            turn(0)
            dt_proj(0)
            for j in range(NBC):
                spread(0, j)
                readout(1, 2 * j, 2)
            in_proj(1)
            sum_states(0)
            sum_states(1)
            x_proj(1)
            sum_states(2)
            turn(1)
            dt_proj(1)
            sum_states(3)
            sum_states(4)
            for j in range(NBC):
                spread(1, j)
                if j == 3:
                    sum_states(5)
            sum_states(6)
            sum_states(7)
            out_proj(0)
            router(0)
            gate_up(0, 0)
            for p in range(1, PAIRS):
                gate_up(0, p, 0)
                turn_h(0, p - 1)
                gate_up(0, p, 1)
                down(0, p - 1)
            turn_h(0, PAIRS - 1)
            down(0, PAIRS - 1)
            out_proj(1)
            router(1)
            gate_up(1, 0)
            for p in range(1, PAIRS):
                gate_up(1, p, 0)
                turn_h(1, p - 1)
                gate_up(1, p, 1)
                down(1, p - 1)
            turn_h(1, PAIRS - 1)
            down(1, PAIRS - 1)

def kernel(**inputs):
    import numpy as np
    import concourse.bacc as bacc
    from concourse.bass_utils import run_bass_kernel_spmd as run

    a = {k: np.asarray(v) for k, v in inputs.items()}
    C = a["L0_attn_out_proj_w"].shape[0]
    chan = np.concatenate([a["L0_attn_conv_w"][:, 0, :], a["L0_attn_conv_b"][:, None],
                           a["L0_attn_dt_proj_b"][:, None], a["L0_attn_D_param"][:, None],
                           a["L0_attn_A_log"]], axis=1)
    chan = chan.reshape(C // 128, 128, -1).transpose(1, 0, 2)
    E, I2, D = a["L0_ffn_w13"].shape
    I = I2 // 2
    sw13 = a["L0_ffn_sw13"].reshape(2, 2, I, D).transpose(1, 0, 2, 3).reshape(2, I2, D)
    w13 = np.concatenate([a["L0_ffn_w13"], sw13], axis=0).reshape(-1, 2, I2, D).transpose(0, 3, 1, 2)
    w2 = np.concatenate([a["L0_ffn_w2"].transpose(0, 2, 1).reshape(-1, D), a["L0_ffn_sw2"].T], axis=0)
    arrays = {
        "x": a["x"], "ctx_t": a["ctx_2048"].transpose(0, 2, 1), "ctx_n": a["ctx_2048"],
        "mask": a["mask_BxS2_bk0"].reshape(1, -1), "in_w": a["L0_attn_in_proj_w"], "chan": chan,
        "x_w": a["L0_attn_x_proj_w"], "dt_w": a["L0_attn_dt_proj_w"], "out_w": a["L0_attn_out_proj_w"],
        "gate_w": a["L0_ffn_gate_w"].T, "w13": w13, "w2": w2,
    }
    arrays = {k: np.ascontiguousarray(v) for k, v in arrays.items()}
    nc = bacc.Bacc("TRN2", target_bir_lowering=False, num_devices=1)
    args = [nc.dram_tensor(f"in_{k}", v.shape, mybir.dt.from_np(v.dtype), kind="ExternalInput").ap()
            for k, v in arrays.items()]
    out = nc.dram_tensor("out_0", a["x"].shape, F32, kind="ExternalOutput").ap()
    build(nc, *args, out)
    r = run(nc, [{f"in_{k}": v for k, v in arrays.items()}], core_ids=[0])
    return r.results[0]["out_0"]
```

```python
from contextlib import ExitStack

import concourse.bass as bass
from concourse import mybir

F32 = mybir.dt.float32
F32R = mybir.dt.float32r
BF16 = mybir.dt.bfloat16
U8 = mybir.dt.uint8
ALU = mybir.AluOpType
ACT = mybir.ActivationFunctionType
AX = mybir.AxisListType

def build(nc, x, ctx_t, ctx_n, mask, in_w, chan, x_w, dt_w, out_w, gate_w, w13, w2, out):
    P = 128
    B, T, D = x.shape
    KEYS = ctx_n.shape[1]
    KD = D // P
    KB = KEYS // 512
    C = out_w.shape[0]
    CT = C // P
    R = dt_w.shape[0]
    N = (x_w.shape[1] - R) // 2
    TAPS = 4
    E = gate_w.shape[1]
    PAIRS = w13.shape[0]
    I = w13.shape[3] // 2
    TOPK = 6
    HC = [(0, P), (P, P), (2 * P, 2 * I - 2 * P)]
    SCALE = float(D) ** -0.5
    LN_EPS, RMS_EPS = 1e-5, 1e-6
    MASKED = -1e30
    NBC = 2 * N * T // 512

    with ExitStack() as ctx:
        def sb(name, shape, dt=F32):
            return ctx.enter_context(nc.sbuf_tensor(name, shape, dt))

        def psum(name, shape, dt=F32):
            return ctx.enter_context(nc.psum_tensor(name, shape, dt))

        def sem(name):
            return ctx.enter_context(nc.semaphore(name))

        work = psum("work", [P, 4, 512])
        tr_ps = psum("tr_ps", [P, 512])
        xt_ps = psum("xt_ps", [P, 512])
        tok_ps = psum("tok_ps", [P, 512])
        acc_ps = psum("acc_ps", [P, 512])
        ro_ps = tok_ps[:, 0:D]
        op_ps = tok_ps[:, D:2 * D]
        lg_ps = xt_ps[:, 256:256 + E]
        xp_ps = xt_ps[:, D:D + R + 2 * N]
        h_ps = acc_ps
        z_ps = acc_ps
        gate_ps = tr_ps
        dtT_ps = tr_ps[:, 0:T]
        partsT_ps = tr_ps[0:6 * N, T:T + T // 2].bitcast(BF16)
        bc_ps = [tr_ps, acc_ps]

        w13_len = PAIRS * KD * 4 * I
        w2_len = PAIRS * 3 * D
        big = sb("big", [P, w13_len + w2_len])
        ctx_len = KD * KEYS

        def ctxT_sb(b):
            return big[:, 2 * b * ctx_len:(2 * b + 1) * ctx_len].rearrange("p (c k) -> p c k", c=KD)

        def ctxN_sb(b):
            return big[:, (2 * b + 1) * ctx_len:(2 * b + 2) * ctx_len].rearrange("p (c d) -> p c d", d=D)

        def w13_sb(p):
            n = KD * 4 * I
            return big[:, p * n:(p + 1) * n].rearrange("p (c e i) -> p c e i", c=KD, e=2)

        def w2_off(p):
            return w13_len + (PAIRS - 1 - p) * 3 * D

        def w2_sb(p):
            return big[:, w2_off(p):w2_off(p) + 3 * D].rearrange("p (c d) -> p c d", c=3)

        inw_sb = sb("inw_sb", [P, KD, 2 * C])
        xw_sb = sb("xw_sb", [P, CT, R + 2 * N])
        dtw_sb = sb("dtw_sb", [P, C])
        outw_sb = sb("outw_sb", [P, CT, D])
        gw_sb = sb("gw_sb", [P, KD, E])
        NCH = TAPS + 3 + N
        chan_sb = sb("chan_sb", [P, CT, NCH])
        half_sb = sb("half_sb", [P, CT, TAPS + 1])
        negA_sb = sb("negA_sb", [P, CT, N])
        ones_bf = sb("ones_bf", [1, P], BF16)
        ident = sb("ident", [P, P])
        ident_bf = sb("ident_bf", [P, P], BF16)
        pick = sb("pick", [3 * 2 * N, 2 * N], BF16)
        tmp_pick = sb("tmp_pick", [3 * 2 * N, 2 * N])
        neghalf = sb("neghalf", [P, 3])
        idle = sb("idle", [P, B])

        x_sb = sb("x_sb", [P, B, D])
        x1_sb = sb("x1_sb", [P, B, D])
        x2_sb = sb("x2_sb", [P, B, D])
        fin_sb = x1_sb
        stats = sb("stats", [P, B, 3, 6])
        mv = sb("mv", [P, B, 3, 2])
        ve = sb("ve", [P, B, 3])
        rstd = sb("rstd", [P, B, 3])
        xn_sb = sb("xn_sb", [P, B, D])
        xT_sb = sb("xT_sb", [P, B, KD, T])

        probs = sb("probs", [P, 2, KEYS])
        p_sb = probs[:, 0, :]
        pT_sb = probs[:, 1, :].rearrange("p (c t) -> p c t", t=T)
        bc0 = sb("bc0", [P, 2 * N * T])
        bc_sb = [bc0[:, :], probs[:, :, :].rearrange("p a k -> p (a k)")]
        mx4 = sb("mx4", [P, B, KB])
        mx = sb("mx", [P, B])
        nm = sb("nm", [P, B])
        valid = sb("valid", [P, B])
        sum4 = sb("sum4", [P, B, KB])
        rsum = sb("rsum", [P, B])
        rinv = sb("rinv", [P, B])
        rvalid = sb("rvalid", [P, B])

        hpad = sb("hpad", [P, CT, T + TAPS - 1])
        cg = sb("cg", [P, CT, T])
        th = sb("th", [P, CT, T])
        thg = sb("thg", [P, CT, T])
        z_sb = sb("z_sb", [P, CT, T])
        u_sb = sb("u_sb", [P, B, CT, T])
        sg_sb = sb("sg_sb", [P, B, CT, T])
        dt_sb = sb("dt_sb", [P, B, CT, T])
        dtu_sb = sb("dtu_sb", [P, B, CT, T])
        ss = sb("ss", [P, B, 3])
        sse = sb("sse", [P, B, 3])
        rr = sb("rr", [P, B, 3])
        dtn = sb("dtn", [P, R])
        dtT = sb("dtT", [P, T])
        bcn = sb("bcn", [P, 2, N])
        bcr = sb("bcr", [P, 2, N])
        parts = sb("parts", [P, 3, 2, N], BF16)
        partsT = sb("partsT", [3 * 2 * N, T], BF16)

        NH = N // 2
        with ExitStack() as scan_room:
            dA = scan_room.enter_context(nc.sbuf_tensor("dA", [P, 4, NH, T], F32))
            st = scan_room.enter_context(nc.sbuf_tensor("st", [P, 4, NH, T], F32))
        n13 = KD * 4 * I
        w13_hi = sb("w13_hi", [P, 3, n13], F32R)
        w13_lo = sb("w13_lo", [P, 2, n13], F32R)
        x_hi = sb("x_hi", [P, D], F32R)
        x_lo = sb("x_lo", [P, D], F32R)
        sb("scan_rest", [P, 2 * 4 * NH * T - 5 * n13 - 2 * D])
        mask_u8 = st[0:1, 0:2].rearrange("p k n t -> p (k n t)")[:, 0:B * KEYS // 4].bitcast(U8)
        y_sb = sb("y_sb", [P, T])
        y2_sb = sb("y2_sb", [P, T])

        ffn_buf = sb("ffn_buf", [P, 8 * I + 6 * P])
        tg = ffn_buf[:, 0:4 * I].rearrange("p (k i) -> p k i", k=4)
        h_sb = ffn_buf[:, 4 * I:8 * I].rearrange("p (k i) -> p k i", k=2)
        hT = ffn_buf[:, 8 * I:8 * I + 6 * P].rearrange("p (k c) -> p k c", k=2)
        up_w = bc0[:, 0:4 * I].rearrange("p (k i) -> p k i", k=4)
        h0_sb = bc0[:, 4 * I:10 * I].rearrange("p (k i) -> p k i", k=3)
        mask_sb = ffn_buf[0:1, 0:B * KEYS // 2].bitcast(BF16)
        nlg = sb("nlg", [P, B])
        ex = sb("ex", [P, E])
        exs = sb("exs", [P, 1])
        exr = sb("exr", [P, 1])
        sc = sb("sc", [P, E + 2])
        rep = sb("rep", [P, E + 2])
        v8 = sb("v8", [P, 8])
        chosen = sb("chosen", [P, E])
        tks = sb("tks", [P, 1])
        tke = sb("tke", [P, 1])
        tkr = sb("tkr", [P, 1])
        cw = sb("cw", [P, B, E + 2])

        ld_x, ld_mask, ld_inw, ld_chan = sem("ld_x"), sem("ld_mask"), sem("ld_inw"), sem("ld_chan")
        ld_xw, ld_dtw, ld_outw, ld_gw = sem("ld_xw"), sem("ld_dtw"), sem("ld_outw"), sem("ld_gw")
        ld_ctxT = [[sem(f"ld_ctxT{b}{j}") for j in range(KB)] for b in range(B)]
        ld_ctxN = [[sem(f"ld_ctxN{b}{j}") for j in range(2)] for b in range(B)]
        ld_ffn = [sem(f"ld_ffn{p}") for p in range(PAIRS)]
        stored = sem("stored")
        s = {}
        for name in """zeroed ident_ready ident_bf_ready pick_half pick_ready mask_ready ones_ready consts_ready
                half_ready A_exp A_ready pads_ready dA0_ready
                scores_ready max4_done max_done nm_ready valid_ready probs_ready pT_psum pT_act pT_dve
                readout_ready sum_done rinv_done rvalid_ready x1_ready
                h_ready gate_ready hpad_ready tap0_done tap_done tanh_h u_ready tanh_g sg_ready
                xp_ready ss_ready sse_ready rr_ready dtn_ready bcn_ready part0 rest1 part1 part2
                dtT_psum dtT_ready partsT_psum partsT_ready z_psum z_ready abs_ready e_ready w_ready nc_ready
                ln_ready q_ready dt_ready dtu_ready bc_psum bc_even bc_odd y_psum folded
                dA_ready dBu_ready scan_done mulC_done dBu_dve mulC_pool y_ready y2_ready yg_ready
                op_ready x2_ready
                lg_ready nlg_ready ex_ready exr_ready sc_ready v8_ready v8s_ready tks_ready rep_ready chosen_ready
                tke_ready tkr_ready cw_ready cw_const sentinel
                gu_ready tg_ready up_ready t1_ready prod_ready hi_ready lo_dve lo_pool x_hi_ready x_lo_ready
                hf_ready tr_ready hT_ready w2_done fin_ready""".split():
            s[name] = sem(name)
        bn_done, var_ready, ve_ready = sem("bn_done"), sem("var_ready"), sem("ve_ready")
        rstd_ready, xn_ready, xT_psum, xT_ready = sem("rstd_ready"), sem("xn_ready"), sem("xT_psum"), sem("xT_ready")

        INPUTS_ON_DVE = (0, 15)
        TIMES_C_ON_POOL = (2, 5)

        def input_ready(eng, m):
            if m in INPUTS_ON_DVE:
                eng.wait_ge(s["dBu_dve"], INPUTS_ON_DVE.index(m) + 1)
            else:
                eng.wait_ge(s["dBu_ready"], m + 1 - sum(k < m for k in INPUTS_ON_DVE))

        def times_c_done(eng, m):
            if m in TIMES_C_ON_POOL:
                eng.wait_ge(s["mulC_pool"], TIMES_C_ON_POOL.index(m) + 1)
            else:
                eng.wait_ge(s["mulC_done"], m + 1 - sum(k < m for k in TIMES_C_ON_POOL))

        def state_used(eng, m):
            k = m // 2
            if k < CT:
                eng.wait_ge(s["y_psum"], m + 1)
            elif m % 2:
                eng.wait_ge(s["folded"], k - CT + 1)
            else:
                eng.wait_ge(s["y_ready"], k - CT + 1)

        def pT_copied(eng, b, j):
            eng.wait_ge(s["pT_dve" if j < KB // 2 else "pT_act"], KB // 2 * b + j % (KB // 2) + 1)

        def bc_copied(eng, b, n):
            eng.wait_ge(s["bc_even"], NBC // 2 * b + (n + 1) // 2)
            if n > 1:
                eng.wait_ge(s["bc_odd"], NBC // 2 * b + n // 2)

        DT_PARTS = (slice(0, 1), slice(1, CT))

        def make_input(eng, ops, ready, b, i, half):
            if i <= 1:
                eng.wait_ge(s["dtu_ready"], 2 * b + i + 1)
            if i == 0:
                bc_copied(eng, b, NBC // 4 * (half + 1))
            m = 2 * (CT * b + i) + half
            if m >= 4:
                state_used(eng, m - 4)
            bm = bc_sb[b][:, half * NH * T:(half + 1) * NH * T].rearrange("p (n t) -> p n t", n=NH)
            ops.tensor_tensor(st[:, m % 4], bm, dtu_sb[:, b, i:i + 1, :].to_broadcast([P, NH, T]),
                              ALU.mult).then_inc(ready, 1)

        def multiply_by_c(eng, ops, ready, b, i, half):
            m = 2 * (CT * b + i) + half
            lo = (N + half * NH) * T
            flat = st[:, m % 4].rearrange("p n t -> p (n t)")
            eng.wait_ge(s["scan_done"], m + 1)
            bc_copied(eng, b, NBC // 2 + NBC // 4 * (half + 1))
            ops.tensor_tensor(flat, flat, bc_sb[b][:, lo:lo + NH * T], ALU.mult).then_inc(ready, 1)

        def w13_flat(p):
            return big[:, p * n13:(p + 1) * n13]

        def gate_up_used(eng, k):
            if k < 2 * PAIRS:
                eng.wait_ge(s["t1_ready"], k // 2 + 1)
                eng.wait_ge(s["up_ready"], k + 1)
            else:
                eng.wait_ge(s["hf_ready"], k - 2 * PAIRS + 1)

        def gate_used(eng, k):
            if k < 2 * PAIRS:
                eng.wait_ge(s["prod_ready"], k // 2 + 1)
            else:
                eng.wait_ge(s["hf_ready"], k - 2 * PAIRS + 1)

        block = ctx.enter_context(nc.Block())

        @block.sync
        def _(sp):
            def load_ctx(b):
                src = ctx_t[b].rearrange("(c p) k -> p c k", p=P)
                for j in range(KB):
                    sp.dma_start(ctxT_sb(b)[:, :, j * 512:(j + 1) * 512],
                                 src[:, :, j * 512:(j + 1) * 512]).then_inc(ld_ctxT[b][j], 16)
                nat = ctx_n[b].rearrange("(c p) d -> p c d", p=P)
                half = KEYS // P // 2
                for j in range(2):
                    sp.dma_start(ctxN_sb(b)[:, j * half:(j + 1) * half, :],
                                 nat[:, j * half:(j + 1) * half, :]).then_inc(ld_ctxN[b][j], 16)

            sp.dma_start(x_sb[:, :, :], x.rearrange("b t d -> t b d")).then_inc(ld_x, 16)
            sp.dma_start(mask_u8[:, :], mask).then_inc(ld_mask, 16)
            load_ctx(0)
            sp.dma_start(inw_sb[:, :, :], in_w.rearrange("(c p) n -> p c n", p=P)).then_inc(ld_inw, 16)
            sp.dma_start(chan_sb[:, :, :], chan).then_inc(ld_chan, 16)
            sp.dma_start(xw_sb[:, :, :], x_w.rearrange("(c p) n -> p c n", p=P)).then_inc(ld_xw, 16)
            sp.dma_start(dtw_sb[:, :], dt_w).then_inc(ld_dtw, 16)
            load_ctx(1)
            sp.dma_start(outw_sb[:, :, :], out_w.rearrange("(c p) n -> p c n", p=P)).then_inc(ld_outw, 16)
            sp.dma_start(gw_sb[:, :, :], gate_w.rearrange("(c p) n -> p c n", p=P)).then_inc(ld_gw, 16)

            def load_w13(p):
                sp.dma_start(w13_sb(p), w13[p].rearrange("(c k) e i -> k c e i", k=P)).then_inc(ld_ffn[p], 16)

            def load_w2(p):
                rows = w2[p * 2 * I:(p + 1) * 2 * I, :]
                sp.dma_start(w2_sb(p)[:, 0:2, :],
                             rows[0:2 * P, :].rearrange("(c k) d -> k c d", k=P)).then_inc(ld_ffn[p], 16)
                sp.dma_start(w2_sb(p)[0:HC[2][1], 2, :], rows[2 * P:2 * I, :]).then_inc(ld_ffn[p], 16)

            sp.wait_ge(s["readout_ready"], 1)
            n13 = KD * 4 * I
            early = [p for p in range(PAIRS) if (p + 1) * n13 <= 2 * ctx_len]
            early2 = [p for p in range(PAIRS) if w2_off(p) >= 4 * ctx_len]
            for p in early:
                load_w13(p)
                if p in early2:
                    load_w2(p)
            sp.wait_ge(s["readout_ready"], 2)
            for p in range(PAIRS):
                if p not in early:
                    load_w13(p)
                if p not in early2 or p not in early:
                    load_w2(p)
            for b in range(B):
                sp.wait_ge(s["fin_ready"], b + 1)
                sp.dma_start(out[b], fin_sb[:, b, :]).then_inc(stored, 16)
            sp.wait_ge(stored, 16 * B)

        @block.gpsimd
        def _(pool):
            g = nc.gpsimd
            g.memset(ident[:, :], 0.0).then_inc(s["zeroed"], 1)
            pool.wait_ge(s["zeroed"], 1)
            g.affine_select(out=ident[:, :], in_=ident[:, :], compare_op=ALU.not_equal, fill=1.0, base=0,
                            pattern=[[-1, P]], channel_multiplier=1).then_inc(s["ident_ready"], 1)
            g.memset(neghalf[:, :], -0.5).then_inc(s["consts_ready"], 1)
            pool.wait_ge(s["consts_ready"], 1)

            def rsqrt_var(l, b):
                pool.wait_ge(var_ready, B * l + b + 1)
                g.tensor_scalar(ve[:, b, l:l + 1], mv[:, b, l, 1:2], LN_EPS, None, ALU.add).then_inc(ve_ready, 1)
                pool.wait_ge(ve_ready, B * l + b + 1)
                g.tensor_tensor(rstd[:, b, l:l + 1], ve[:, b, l:l + 1], neghalf[:, 0:1],
                                ALU.pow).then_inc(rstd_ready, 1)

            def rsqrt_rms(b):
                pool.wait_ge(s["ss_ready"], 3 * (b + 1))
                g.tensor_scalar(sse[:, b, :], ss[:, b, :], RMS_EPS, None, ALU.add).then_inc(s["sse_ready"], 1)
                pool.wait_ge(s["sse_ready"], b + 1)
                g.tensor_tensor(rr[:, b, :], sse[:, b, :], neghalf[:, :], ALU.pow).then_inc(s["rr_ready"], 1)

            def inputs(b, i, half):
                make_input(pool, g, s["dBu_ready"], b, i, half)

            def times_c(b, i, half):
                multiply_by_c(pool, g, s["mulC_pool"], b, i, half)

            def fold(i):
                m = 2 * (CT + i)
                times_c_done(pool, m)
                times_c_done(pool, m + 1)
                g.tensor_tensor(st[:, m % 4], st[:, m % 4], st[:, (m + 1) % 4], ALU.add).then_inc(s["folded"], 1)

            def low(p):
                pool.wait_ge(s["hi_ready"], p + 1)
                if p >= 2:
                    pool.wait_ge(s["gu_ready"], 2 * (PAIRS + p - 2) + 2)
                g.tensor_tensor(w13_lo[:, p % 2, n13 // 2:n13], w13_flat(p)[:, n13 // 2:n13], w13_hi[:, p % 3, n13 // 2:n13].bitcast(F32),
                                ALU.subtract).then_inc(s["lo_pool"], 1)

            def product(p):
                pool.wait_ge(s["t1_ready"], p + 1)
                pool.wait_ge(s["up_ready"], 2 * p + 2)
                if p >= 3:
                    pool.wait_ge(s["tr_ready"], p - 2)
                k = 2 * p % 4
                g.tensor_tensor(h0_sb[:, p % 3].rearrange("p (e i) -> p e i", e=2), tg[:, k:k + 2, :],
                                up_w[:, k:k + 2, :], ALU.mult).then_inc(s["prod_ready"], 1)

            rsqrt_var(0, 0)
            rsqrt_var(0, 1)
            rsqrt_var(1, 0)
            rsqrt_rms(0)
            inputs(0, 0, 1)
            rsqrt_var(1, 1)
            inputs(0, 1, 0)
            inputs(0, 1, 1)
            times_c(0, 1, 0)
            inputs(0, 2, 0)
            rsqrt_rms(1)
            inputs(0, 2, 1)
            inputs(0, 3, 0)
            inputs(0, 3, 1)
            times_c(0, 2, 1)
            inputs(1, 0, 0)
            inputs(1, 0, 1)
            inputs(1, 1, 0)
            inputs(1, 1, 1)
            rsqrt_var(2, 0)
            fold(0)
            inputs(1, 2, 0)
            product(0)
            inputs(1, 2, 1)
            product(1)
            fold(1)
            product(2)
            inputs(1, 3, 0)
            fold(2)
            for j in range(3, 6):
                product(j)
            fold(3)
            product(6)
            product(7)
            low(0)
            rsqrt_var(2, 1)
            low(1)
            product(8)
            for p in range(2, PAIRS):
                low(p)

        @block.scalar
        def _(act):
            a = nc.scalar

            def xT_copy(l, b):
                act.wait_ge(xT_psum, B * l + b + 1)
                a.copy(xT_sb[:, b].rearrange("p c t -> p (c t)"), xt_ps[:, 0:D]).then_inc(xT_ready, 1)

            def softmax_exp(b):
                act.wait_ge(s["nm_ready"], b + 1)
                for j in range(KB):
                    a.activation(p_sb[:, j * 512:(j + 1) * 512], work[:, j, :], ACT.Exp, bias=nm[:, b:b + 1],
                                 scale=SCALE, accum_out=sum4[:, b, j:j + 1]).then_inc(s["probs_ready"], 1)

            def pT_copy(b, j):
                act.wait_ge(s["pT_psum"], KB * b + j + 1)
                a.copy(probs[:, 1, j * 512:(j + 1) * 512], work[:, j, :]).then_inc(s["pT_act"], 1)

            def gate_tanh(b):
                if b:
                    act.wait_ge(s["dt_ready"], 2 * b)
                act.wait_ge(s["gate_ready"], b + 1)
                a.activation(thg[:, :, :].rearrange("p c t -> p (c t)"), gate_ps[:, :], ACT.Tanh,
                             scale=0.5).then_inc(s["tanh_g"], 1)

            def conv_head(b):
                if b:
                    act.wait_ge(s["dt_ready"], 2 * b)
                act.wait_ge(s["h_ready"], b + 1)
                a.copy(hpad[:, :, TAPS - 1:], h_ps[:, :].rearrange("p (c t) -> p c t", c=CT))\
                    .then_inc(s["hpad_ready"], 1)
                act.wait_ge(s["half_ready"], 1)
                act.wait_ge(s["hpad_ready"], b + 1)
                for i in range(CT):
                    a.activation(cg[:, i, :], hpad[:, i, TAPS - 1:], ACT.Identity, scale=half_sb[:, i, TAPS - 1:TAPS],
                                 bias=half_sb[:, i, TAPS:TAPS + 1]).then_inc(s["tap0_done"], 1)

            def conv_tanh(b):
                act.wait_ge(s["tap_done"], (TAPS - 1) * CT * (b + 1))
                a.activation(th[:, :, :], cg[:, :, :], ACT.Tanh).then_inc(s["tanh_h"], 1)

            def squares(b):
                act.wait_ge(s["xp_ready"], b + 1)
                for k, (lo, n) in enumerate([(0, R), (R, N), (R + N, N)]):
                    a.activation(z_sb[:, k, 0:n], xp_ps[:, lo:lo + n], ACT.Square, scale=float(n) ** -0.5,
                                 accum_out=ss[:, b, k:k + 1]).then_inc(s["ss_ready"], 1)

            def softplus_exp(b):
                act.wait_ge(s["z_ready"], b + 1)
                a.activation(th[:, :, :], z_sb[:, :, :], ACT.Abs).then_inc(s["abs_ready"], 1)
                act.wait_ge(s["abs_ready"], b + 1)
                a.activation(thg[:, :, :], th[:, :, :], ACT.Exp, scale=-1.0).then_inc(s["e_ready"], 1)

            def softplus_ln(b):
                act.wait_ge(s["w_ready"], b + 1)
                for part in DT_PARTS:
                    a.activation(th[:, part, :], cg[:, part, :], ACT.Ln).then_inc(s["ln_ready"], 1)

            def load_exp(b):
                a.activation(idle[:, b:b + 1], neghalf[:, 0:1], ACT.Exp)

            def bc_copy(b, j):
                act.wait_ge(s["bc_psum"], NBC * b + j + 1)
                a.copy(bc_sb[b][:, j * 512:(j + 1) * 512], bc_ps[j % 2][:, :])\
                    .then_inc(s["bc_odd" if j % 2 else "bc_even"], 1)

            def decays(b, i, half):
                m = 2 * (CT * b + i) + half
                if i <= 1:
                    act.wait_ge(s["dt_ready"], 2 * b + i + 1)
                if m >= 4:
                    act.wait_ge(s["scan_done"], m - 3)
                for n in range(NH):
                    nn = half * NH + n
                    last = a.activation(dA[:, m % 4, n, 1:T], dt_sb[:, b, i, 1:T], ACT.Exp,
                                        scale=negA_sb[:, i, nn:nn + 1])
                last.then_inc(s["dA_ready"], 1)

            def gate_exp(b):
                act.wait_ge(s["nlg_ready"], b + 1)
                a.activation(ex[:, :], lg_ps, ACT.Exp, bias=nlg[:, b:b + 1],
                             accum_out=exs[:, :]).then_inc(s["ex_ready"], 1)

            def ffn_tanh(b, p, *es):
                for e in es or range(2):
                    k = 2 * (PAIRS * b + p) + e
                    act.wait_ge(s["gu_ready"], k + 1)
                    if k >= 4:
                        gate_used(act, k - 4)
                    a.activation(tg[:, k % 4, :], work[:, k % 4, 0:I], ACT.Tanh, scale=0.5).then_inc(s["tg_ready"], 1)
                    if not b:
                        if k == 0:
                            act.wait_ge(s["cw_ready"], 1)
                            act.wait_ge(s["cw_const"], 1)
                        a.activation(up_w[:, k % 4, :], work[:, k % 4, I:2 * I], ACT.Identity,
                                     scale=cw[:, 0, k:k + 1]).then_inc(s["up_ready"], 1)

            def high(p):
                if p < 3:
                    act.wait_ge(s["yg_ready"], 2 * CT)
                else:
                    act.wait_ge(s["gu_ready"], 2 * (PAIRS + p - 3) + 2)
                act.wait_ge(ld_ffn[p], 48)
                a.copy(w13_hi[:, p % 3, :], w13_flat(p)).then_inc(s["hi_ready"], 1)

            def x_high():
                act.wait_ge(xT_ready, 2 * B + 2)
                a.copy(x_hi[:, :], xT_sb[:, 1].rearrange("p c t -> p (c t)")).then_inc(s["x_hi_ready"], 1)

            def hT_copy(b, p):
                k = PAIRS * b + p
                act.wait_ge(s["tr_ready"], k + 1)
                if k >= 2:
                    act.wait_ge(s["w2_done"], k - 1)
                a.copy(hT[:, k % 2, 0:2 * P], tr_ps[:, 0:2 * P]).then_inc(s["hT_ready"], 1)
                m = HC[2][1]
                a.copy(hT[0:m, k % 2, 2 * P:3 * P], tr_ps[0:m, 2 * P:3 * P]).then_inc(s["hT_ready"], 1)

            xT_copy(0, 0)
            xT_copy(0, 1)
            softmax_exp(0)
            pT_copy(0, 2)
            pT_copy(0, 3)
            act.wait_ge(ld_chan, 16)
            a.activation(negA_sb[:, :, :], chan_sb[:, :, TAPS + 3:NCH], ACT.Exp).then_inc(s["A_exp"], 1)
            xT_copy(1, 0)
            act.wait_ge(s["pads_ready"], 1)
            conv_head(0)
            gate_tanh(0)
            conv_tanh(0)
            squares(0)
            softmax_exp(1)
            pT_copy(1, 2)
            pT_copy(1, 3)
            softplus_exp(0)
            softplus_ln(0)
            bc_copy(0, 3)
            act.wait_ge(s["consts_ready"], 1)
            load_exp(0)
            act.wait_ge(s["A_ready"], 1)
            act.wait_ge(s["dA0_ready"], 4)
            decays(0, 0, 0)
            bc_copy(0, 4)
            bc_copy(0, 5)
            decays(0, 0, 1)
            bc_copy(0, 6)
            bc_copy(0, 7)
            xT_copy(1, 1)
            decays(0, 1, 0)
            conv_head(1)
            gate_tanh(1)
            decays(0, 1, 1)
            conv_tanh(1)
            decays(0, 2, 0)
            squares(1)
            decays(0, 2, 1)
            decays(0, 3, 0)
            bc_copy(1, 0)
            softplus_exp(1)
            bc_copy(1, 1)
            softplus_ln(1)
            bc_copy(1, 2)
            bc_copy(1, 3)
            decays(0, 3, 1)
            decays(1, 0, 0)
            decays(1, 0, 1)
            load_exp(1)
            bc_copy(1, 5)
            bc_copy(1, 6)
            decays(1, 1, 0)
            bc_copy(1, 7)
            decays(1, 1, 1)
            xT_copy(2, 0)
            decays(1, 2, 0)
            gate_exp(0)
            ffn_tanh(0, 0, 0)
            ffn_tanh(0, 0, 1)
            ffn_tanh(0, 1, 0)
            ffn_tanh(0, 1, 1)
            decays(1, 2, 1)
            hT_copy(0, 0)
            ffn_tanh(0, 2, 0)
            ffn_tanh(0, 2, 1)
            decays(1, 3, 0)
            hT_copy(0, 1)
            ffn_tanh(0, 3, 0)
            ffn_tanh(0, 3, 1)
            decays(1, 3, 1)
            hT_copy(0, 2)
            ffn_tanh(0, 4, 0)
            ffn_tanh(0, 4, 1)
            hT_copy(0, 3)
            ffn_tanh(0, 5, 0)
            ffn_tanh(0, 5, 1)
            ffn_tanh(0, 6, 0)
            hT_copy(0, 4)
            hT_copy(0, 5)
            ffn_tanh(0, 6, 1)
            ffn_tanh(0, 7, 0)
            ffn_tanh(0, 7, 1)
            high(0)
            high(1)
            hT_copy(0, 6)
            ffn_tanh(0, 8, 0)
            ffn_tanh(0, 8, 1)
            xT_copy(2, 1)
            hT_copy(0, 7)
            x_high()
            high(2)
            hT_copy(0, 8)
            gate_exp(1)
            ffn_tanh(1, 0)
            for p in range(1, PAIRS):
                ffn_tanh(1, p, 0)
                hT_copy(1, p - 1)
                ffn_tanh(1, p, 1)
                if p + 2 < PAIRS:
                    high(p + 2)
            hT_copy(1, PAIRS - 1)

        @block.vector
        def _(dve):
            v = nc.vector

            def ln_stats(l, b, src):
                v.bn_stats(stats[:, b, l, :], src).then_inc(bn_done, 1)
                dve.wait_ge(bn_done, B * l + b + 1)
                v.bn_aggr(mv[:, b, l, :], stats[:, b, l, :]).then_inc(var_ready, 1)

            def ln_apply(l, b, src):
                if l:
                    dve.wait_ge(xT_psum, B * (l - 1) + b + 1)
                dve.wait_ge(rstd_ready, B * l + b + 1)
                v.tensor_scalar(xn_sb[:, b, :], src, mv[:, b, l, 0:1], rstd[:, b, l:l + 1],
                                ALU.subtract, ALU.mult).then_inc(xn_ready, 1)

            def norm1(b):
                ln_apply(1, b, x1_sb[:, b, :])

            def norm2(b):
                ln_apply(2, b, x2_sb[:, b, :])

            def bank_max(b, j):
                dve.wait_ge(s["scores_ready"], KB * b + j + 1)
                v.reduce_max(mx4[:, b, j:j + 1], work[:, j, :], AX.X).then_inc(s["max4_done"], 1)

            def row_max(b):
                dve.wait_ge(s["max4_done"], KB * (b + 1))
                v.reduce_max(mx[:, b:b + 1], mx4[:, b, :], AX.X).then_inc(s["max_done"], 1)
                dve.wait_ge(s["max_done"], b + 1)
                v.tensor_scalar(nm[:, b:b + 1], mx[:, b:b + 1], -SCALE, None, ALU.mult).then_inc(s["nm_ready"], 1)
                v.tensor_scalar(valid[:, b:b + 1], mx[:, b:b + 1], 0.1 * MASKED, None,
                                ALU.is_gt).then_inc(s["valid_ready"], 1)

            def pT_copy(b, j):
                dve.wait_ge(s["pT_psum"], KB * b + j + 1)
                v.tensor_copy(probs[:, 1, j * 512:(j + 1) * 512], work[:, j, :]).then_inc(s["pT_dve"], 1)

            def attn_sums(b):
                dve.wait_ge(s["probs_ready"], KB * (b + 1))
                v.reduce_sum(rsum[:, b:b + 1], sum4[:, b, :], AX.X).then_inc(s["sum_done"], 1)
                dve.wait_ge(s["sum_done"], b + 1)
                v.reciprocal(rinv[:, b:b + 1], rsum[:, b:b + 1]).then_inc(s["rinv_done"], 1)
                dve.wait_ge(s["rinv_done"], b + 1)
                dve.wait_ge(s["valid_ready"], b + 1)
                v.tensor_tensor(rvalid[:, b:b + 1], rinv[:, b:b + 1], valid[:, b:b + 1],
                                ALU.mult).then_inc(s["rvalid_ready"], 1)

            def residual1(b):
                dve.wait_ge(s["readout_ready"], b + 1)
                dve.wait_ge(s["rvalid_ready"], b + 1)
                v.scalar_tensor_tensor(out=x1_sb[:, b, :], in0=ro_ps, scalar=rvalid[:, b:b + 1],
                                       in1=x_sb[:, b, :], op0=ALU.mult, op1=ALU.add).then_inc(s["x1_ready"], 1)
                dve.wait_ge(s["x1_ready"], b + 1)
                ln_stats(1, b, x1_sb[:, b, :])

            def conv(b):
                dve.wait_ge(s["hpad_ready"], b + 1)
                for k in range(TAPS - 1):
                    for i in range(CT):
                        if k:
                            dve.wait_ge(s["tap_done"], CT * ((TAPS - 1) * b + k - 1) + i + 1)
                        else:
                            dve.wait_ge(s["tap0_done"], CT * b + i + 1)
                        v.scalar_tensor_tensor(out=cg[:, i, :], in0=hpad[:, i, k:k + T],
                                               scalar=half_sb[:, i, k:k + 1], in1=cg[:, i, :],
                                               op0=ALU.mult, op1=ALU.add).then_inc(s["tap_done"], 1)
                dve.wait_ge(s["tanh_g"], b + 1)
                v.scalar_tensor_tensor(out=sg_sb[:, b].rearrange("p c t -> p (c t)"),
                                       in0=thg[:, :, :].rearrange("p c t -> p (c t)"), scalar=1.0,
                                       in1=gate_ps[:, :], op0=ALU.add, op1=ALU.mult).then_inc(s["sg_ready"], 1)
                dve.wait_ge(s["tanh_h"], b + 1)
                v.scalar_tensor_tensor(out=u_sb[:, b], in0=th[:, :, :], scalar=1.0, in1=cg[:, :, :],
                                       op0=ALU.add, op1=ALU.mult).then_inc(s["u_ready"], 1)

            def normed(b):
                dve.wait_ge(s["rr_ready"], b + 1)
                v.tensor_scalar(dtn[:, :], xp_ps[:, 0:R], rr[:, b, 0:1], None, ALU.mult)\
                    .then_inc(s["dtn_ready"], 1)
                v.tensor_tensor(bcn[:, :, :], xp_ps[:, R:R + 2 * N].rearrange("p (a n) -> p a n", a=2),
                                rr[:, b, 1:3].unsqueeze(2).to_broadcast([P, 2, N]),
                                ALU.mult).then_inc(s["bcn_ready"], 1)

            def bc_high(b):
                dve.wait_ge(s["bcn_ready"], b + 1)
                v.tensor_copy(parts[:, 0], bcn[:, :, :]).then_inc(s["part0"], 1)
                dve.wait_ge(s["part0"], b + 1)
                v.tensor_tensor(bcr[:, :, :], bcn[:, :, :], parts[:, 0], ALU.subtract).then_inc(s["rest1"], 1)

            def bc_low(b):
                dve.wait_ge(s["rest1"], b + 1)
                v.tensor_copy(parts[:, 1], bcr[:, :, :]).then_inc(s["part1"], 1)
                dve.wait_ge(s["part1"], b + 1)
                v.tensor_tensor(parts[:, 2], bcr[:, :, :], parts[:, 1], ALU.subtract).then_inc(s["part2"], 1)

            def dtT_copy(b):
                dve.wait_ge(s["dtT_psum"], b + 1)
                v.tensor_copy(dtT[:, :], dtT_ps).then_inc(s["dtT_ready"], 1)

            def partsT_copy(b):
                dve.wait_ge(s["partsT_psum"], b + 1)
                v.tensor_copy(partsT[:, :], partsT_ps).then_inc(s["partsT_ready"], 1)

            def dt_bias(b):
                dve.wait_ge(s["z_psum"], b + 1)
                v.tensor_tensor(z_sb[:, :, :], z_ps[:, :].rearrange("p (c t) -> p c t", c=CT),
                                chan_sb[:, :, TAPS + 1:TAPS + 2].to_broadcast([P, CT, T]),
                                ALU.add).then_inc(s["z_ready"], 1)

            def bc_copy(b, j):
                dve.wait_ge(s["bc_psum"], NBC * b + j + 1)
                v.tensor_copy(bc_sb[b][:, j * 512:(j + 1) * 512], bc_ps[j % 2][:, :])\
                    .then_inc(s["bc_odd" if j % 2 else "bc_even"], 1)

            def softplus_w(b):
                dve.wait_ge(s["e_ready"], b + 1)
                v.tensor_scalar(cg[:, :, :], thg[:, :, :], 1.0, None, ALU.add).then_inc(s["w_ready"], 1)

            def softplus_rounding(b):
                dve.wait_ge(s["w_ready"], b + 1)
                v.scalar_tensor_tensor(out=thg[:, :, :], in0=cg[:, :, :], scalar=-1.0, in1=thg[:, :, :],
                                       op0=ALU.add, op1=ALU.subtract).then_inc(s["nc_ready"], 1)

            def softplus_base(b):
                dve.wait_ge(s["nc_ready"], b + 1)
                v.scalar_tensor_tensor(out=z_sb[:, :, :], in0=z_sb[:, :, :], scalar=0.0, in1=thg[:, :, :],
                                       op0=ALU.max, op1=ALU.subtract).then_inc(s["q_ready"], 1)

            def softplus_dt(b, k):
                dve.wait_ge(s["q_ready"], b + 1)
                dve.wait_ge(s["ln_ready"], 2 * b + k + 1)
                part = DT_PARTS[k]
                v.tensor_tensor(dt_sb[:, b, part], z_sb[:, part, :], th[:, part, :], ALU.add)\
                    .then_inc(s["dt_ready"], 1)

            def softplus_dtu(b, k):
                dve.wait_ge(s["dt_ready"], 2 * b + k + 1)
                part = DT_PARTS[k]
                v.tensor_tensor(dtu_sb[:, b, part], dt_sb[:, b, part], u_sb[:, b, part], ALU.mult)\
                    .then_inc(s["dtu_ready"], 1)

            def recur(b, i, half):
                m = 2 * (CT * b + i) + half
                flat = st[:, m % 4].rearrange("p n t -> p (n t)")
                dve.wait_ge(s["dA_ready"], m + 1)
                input_ready(dve, m)
                v.tensor_tensor_scan(flat, dA[:, m % 4].rearrange("p n t -> p (n t)"), flat, 0.0,
                                     ALU.mult, ALU.add).then_inc(s["scan_done"], 1)

            def inputs(b, i, half):
                make_input(dve, v, s["dBu_dve"], b, i, half)

            def times_c(b, i, half):
                multiply_by_c(dve, v, s["mulC_done"], b, i, half)

            def sum_folded(i):
                k = CT + i
                dve.wait_ge(s["folded"], i + 1)
                dve.wait_ge(s["y2_ready"], k)
                v.reduce_sum(y_sb[:, :], st[:, 2 * k % 4].rearrange("p n t -> p t n"), AX.X)\
                    .then_inc(s["y_ready"], 1)

            def gated(b, i):
                k = CT * b + i
                state_used(dve, 2 * k + 1 - b)
                if k:
                    dve.wait_ge(s["yg_ready"], k)
                v.scalar_tensor_tensor(out=y2_sb[:, :], in0=u_sb[:, b, i], scalar=chan_sb[:, i, TAPS + 2:TAPS + 3],
                                       in1=y_sb[:, :] if b else work[:, i, 0:T],
                                       op0=ALU.mult, op1=ALU.add).then_inc(s["y2_ready"], 1)
                dve.wait_ge(s["y2_ready"], k + 1)
                v.scalar_tensor_tensor(out=sg_sb[:, b, i], in0=y2_sb[:, :], scalar=0.5, in1=sg_sb[:, b, i],
                                       op0=ALU.mult, op1=ALU.mult).then_inc(s["yg_ready"], 1)

            def residual2(b):
                dve.wait_ge(s["op_ready"], b + 1)
                v.tensor_tensor(x2_sb[:, b, :], op_ps, x1_sb[:, b, :], ALU.add).then_inc(s["x2_ready"], 1)
                dve.wait_ge(s["x2_ready"], b + 1)
                ln_stats(2, b, x2_sb[:, b, :])

            def route(b):
                dve.wait_ge(s["lg_ready"], b + 1)
                v.tensor_reduce(nlg[:, b:b + 1], lg_ps, AX.X, ALU.max, negate=True).then_inc(s["nlg_ready"], 1)
                dve.wait_ge(s["ex_ready"], b + 1)
                v.reciprocal(exr[:, :], exs[:, :]).then_inc(s["exr_ready"], 1)
                dve.wait_ge(s["exr_ready"], b + 1)
                v.tensor_scalar(sc[:, 0:E], ex[:, :], exr[:, 0:1], None, ALU.mult).then_inc(s["sc_ready"], 1)
                dve.wait_ge(s["sc_ready"], b + 1)
                v.max(v8[:, :], sc[:, :]).then_inc(s["v8_ready"], 1)
                dve.wait_ge(s["v8_ready"], b + 1)
                v.reduce_sum(tks[:, :], v8[:, 0:TOPK], AX.X).then_inc(s["tks_ready"], 1)
                v.tensor_copy(v8[:, TOPK:8], sc[:, E:E + 2]).then_inc(s["v8s_ready"], 1)
                dve.wait_ge(s["v8s_ready"], b + 1)
                v.match_replace(out=rep[:, :], in_to_replace=v8[:, :], in_values=sc[:, :],
                                imm_value=0.0).then_inc(s["rep_ready"], 1)
                dve.wait_ge(s["tks_ready"], b + 1)
                v.tensor_scalar(tke[:, :], tks[:, :], 1e-20, None, ALU.add).then_inc(s["tke_ready"], 1)
                dve.wait_ge(s["tke_ready"], b + 1)
                v.reciprocal(tkr[:, :], tke[:, :]).then_inc(s["tkr_ready"], 1)
                dve.wait_ge(s["rep_ready"], b + 1)
                v.tensor_tensor(chosen[:, :], sc[:, 0:E], rep[:, 0:E], ALU.subtract).then_inc(s["chosen_ready"], 1)
                dve.wait_ge(s["chosen_ready"], b + 1)
                dve.wait_ge(s["tkr_ready"], b + 1)
                v.tensor_scalar(cw[:, b, 0:E], chosen[:, :], tkr[:, 0:1], 0.5, ALU.mult, ALU.mult)\
                    .then_inc(s["cw_ready"], 1)

            def twice_silu(k, n):
                dve.wait_ge(s["tg_ready"], k + n)
                if k < 2 * PAIRS:
                    dve.wait_ge(s["up_ready"], k + n)
                v.scalar_tensor_tensor(out=tg[:, k % 4:k % 4 + n, :], in0=tg[:, k % 4:k % 4 + n, :], scalar=1.0,
                                       in1=work[:, k % 4:k % 4 + n, 0:I], op0=ALU.add, op1=ALU.mult)\
                    .then_inc(s["t1_ready"], 1)

            def low(p):
                dve.wait_ge(s["hi_ready"], p + 1)
                if p >= 2:
                    dve.wait_ge(s["gu_ready"], 2 * (PAIRS + p - 2) + 2)
                v.tensor_tensor(w13_lo[:, p % 2, 0:n13 // 2], w13_flat(p)[:, 0:n13 // 2], w13_hi[:, p % 3, 0:n13 // 2].bitcast(F32),
                                ALU.subtract).then_inc(s["lo_dve"], 1)

            def x_low():
                dve.wait_ge(s["x_hi_ready"], 1)
                v.tensor_tensor(x_lo[:, :], xT_sb[:, 1].rearrange("p c t -> p (c t)"), x_hi[:, :].bitcast(F32),
                                ALU.subtract).then_inc(s["x_lo_ready"], 1)

            def ffn_h(p):
                if p == 0:
                    dve.wait_ge(s["cw_ready"], 2)
                for e in range(2):
                    twice_silu(2 * (PAIRS + p) + e, 1)
                if p >= 2:
                    dve.wait_ge(s["tr_ready"], PAIRS + p - 1)
                for e in range(2):
                    k = 2 * (PAIRS + p) + e
                    dve.wait_ge(s["t1_ready"], PAIRS + 2 * p + e + 1)
                    v.scalar_tensor_tensor(out=h_sb[:, p % 2, e * I:(e + 1) * I], in0=tg[:, k % 4, :],
                                           scalar=cw[:, 1, 2 * p + e:2 * p + e + 1],
                                           in1=work[:, k % 4, I:2 * I], op0=ALU.mult, op1=ALU.mult)\
                        .then_inc(s["hf_ready"], 1)

            def finish(b):
                dve.wait_ge(s["w2_done"], PAIRS * (b + 1))
                v.tensor_tensor(fin_sb[:, b, :], acc_ps[:, b * D:(b + 1) * D], x2_sb[:, b, :],
                                ALU.add).then_inc(s["fin_ready"], 1)

            v.memset(ones_bf[:, :], 1.0).then_inc(s["ones_ready"], 1)
            v.memset(hpad[:, :, 0:TAPS - 1], 0.0).then_inc(s["pads_ready"], 1)
            for k in range(4):
                v.memset(dA[:, k, :, 0:1], 0.0).then_inc(s["dA0_ready"], 1)
            v.memset(cw[:, :, E:E + 2], 0.5).then_inc(s["cw_const"], 1)
            v.memset(sc[:, E:E + 1], -1.0).then_inc(s["sentinel"], 1)
            v.memset(sc[:, E + 1:E + 2], -2.0).then_inc(s["sentinel"], 1)
            dve.wait_ge(ld_x, 16)
            ln_stats(0, 0, x_sb[:, 0, :])
            ln_stats(0, 1, x_sb[:, 1, :])
            ln_apply(0, 0, x_sb[:, 0, :])
            ln_apply(0, 1, x_sb[:, 1, :])
            dve.wait_ge(ld_mask, 16)
            for b in range(B):
                v.tensor_scalar(mask_sb[:, b * KEYS:(b + 1) * KEYS], mask_u8[:, b * KEYS:(b + 1) * KEYS],
                                1.0, -MASKED, ALU.subtract, ALU.mult).then_inc(s["mask_ready"], 1)
            dve.wait_ge(s["ident_ready"], 1)
            v.tensor_copy(ident_bf[:, :], ident[:, :]).then_inc(s["ident_bf_ready"], 1)
            Q = 2 * N
            v.tensor_tensor(tmp_pick[:, :], ident[0:3 * Q, 0:Q], ident[0:3 * Q, Q:2 * Q],
                            ALU.add).then_inc(s["pick_half"], 1)
            dve.wait_ge(s["pick_half"], 1)
            v.tensor_tensor(pick[:, :], tmp_pick[:, :], ident[0:3 * Q, 2 * Q:3 * Q],
                            ALU.add).then_inc(s["pick_ready"], 1)
            for j in range(4):
                bank_max(0, j)
            row_max(0)
            pT_copy(0, 0)
            pT_copy(0, 1)
            attn_sums(0)
            residual1(0)
            norm1(0)
            dve.wait_ge(s["A_exp"], 1)
            v.tensor_scalar(negA_sb[:, :, :], negA_sb[:, :, :], -1.0, None, ALU.mult).then_inc(s["A_ready"], 1)
            dve.wait_ge(ld_chan, 16)
            v.tensor_scalar(half_sb[:, :, :], chan_sb[:, :, 0:TAPS + 1], 0.5, None, ALU.mult)\
                .then_inc(s["half_ready"], 1)
            bank_max(1, 0)
            bank_max(1, 1)
            conv(0)
            bank_max(1, 2)
            bank_max(1, 3)
            row_max(1)
            normed(0)
            bc_high(0)
            dtT_copy(0)
            bc_low(0)
            pT_copy(1, 0)
            partsT_copy(0)
            dt_bias(0)
            pT_copy(1, 1)
            bc_copy(0, 0)
            bc_copy(0, 1)
            softplus_w(0)
            softplus_rounding(0)
            bc_copy(0, 2)
            softplus_base(0)
            softplus_dt(0, 0)
            softplus_dtu(0, 0)
            inputs(0, 0, 0)
            softplus_dt(0, 1)
            attn_sums(1)
            recur(0, 0, 0)
            residual1(1)
            softplus_dtu(0, 1)
            norm1(1)
            times_c(0, 0, 0)
            recur(0, 0, 1)
            times_c(0, 0, 1)
            recur(0, 1, 0)
            conv(1)
            recur(0, 1, 1)
            gated(0, 0)
            times_c(0, 1, 1)
            normed(1)
            bc_high(1)
            bc_low(1)
            dtT_copy(1)
            partsT_copy(1)
            recur(0, 2, 0)
            dt_bias(1)
            recur(0, 2, 1)
            softplus_w(1)
            times_c(0, 2, 0)
            softplus_rounding(1)
            recur(0, 3, 0)
            softplus_base(1)
            softplus_dt(1, 0)
            softplus_dt(1, 1)
            softplus_dtu(1, 0)
            softplus_dtu(1, 1)
            times_c(0, 3, 0)
            bc_copy(1, 4)
            recur(0, 3, 1)
            times_c(0, 3, 1)
            gated(0, 1)
            recur(1, 0, 0)
            gated(0, 2)
            gated(0, 3)
            times_c(1, 0, 0)
            recur(1, 0, 1)
            residual2(0)
            times_c(1, 0, 1)
            norm2(0)
            recur(1, 1, 0)
            times_c(1, 1, 0)
            sum_folded(0)
            dve.wait_ge(s["sentinel"], 2)
            dve.wait_ge(s["cw_const"], 1)
            route(0)
            recur(1, 1, 1)
            twice_silu(0, 2)
            gated(1, 0)
            times_c(1, 1, 1)
            twice_silu(2, 2)
            recur(1, 2, 0)
            recur(1, 2, 1)
            twice_silu(4, 2)
            sum_folded(1)
            times_c(1, 2, 0)
            times_c(1, 2, 1)
            twice_silu(6, 2)
            recur(1, 3, 0)
            gated(1, 1)
            times_c(1, 3, 0)
            twice_silu(8, 2)
            inputs(1, 3, 1)
            sum_folded(2)
            twice_silu(10, 2)
            recur(1, 3, 1)
            times_c(1, 3, 1)
            gated(1, 2)
            twice_silu(12, 2)
            sum_folded(3)
            gated(1, 3)
            twice_silu(14, 2)
            low(0)
            residual2(1)
            norm2(1)
            twice_silu(16, 2)
            low(1)
            x_low()
            route(1)
            finish(0)
            for p in range(PAIRS):
                ffn_h(p)
                if p + 2 < PAIRS:
                    low(p + 2)
            finish(1)

        @block.tensor
        def _(pe):
            t_ = nc.tensor

            def warm_up(n, rhs, bank):
                for _ in range(n):
                    t_.matmul(bank[:, 0:rhs.shape[-1]], ident[:, :], rhs, start=True, stop=True)

            def xT(l, b):
                pe.wait_ge(xn_ready, B * l + b + 1)
                if l == 0 and b == 0:
                    pe.wait_ge(s["ident_ready"], 1)
                for c in range(KD):
                    last = t_.transpose(xt_ps[:, c * P:(c + 1) * P], xn_sb[:, b, c * P:(c + 1) * P], ident[:, :])
                last.then_inc(xT_psum, 1)

            def scores(b, j):
                if j == 0:
                    pe.wait_ge(xT_ready, b + 1)
                if b:
                    pT_copied(pe, b - 1, j)
                pe.wait_ge(ld_ctxT[b][j], 16)
                for c in range(KD):
                    t_.matmul(work[:, j, :], xT_sb[:, b, c, :], ctxT_sb(b)[:, c, j * 512:(j + 1) * 512],
                              start=(c == 0), stop=False)
                if j == 0:
                    pe.wait_ge(s["mask_ready"], b + 1)
                    pe.wait_ge(s["ones_ready"], 1)
                lo = b * KEYS + j * 512
                t_.matmul(work[:, j, :], ones_bf[:, :], mask_sb[:, lo:lo + 512],
                          start=False, stop=True).then_inc(s["scores_ready"], 1)

            def transposes(b, j):
                pe.wait_ge(s["probs_ready"], KB * b + j + 1)
                for c in range(4):
                    lo = j * 512 + c * P
                    last = t_.transpose(work[:, j, c * P:(c + 1) * P], p_sb[:, lo:lo + P], ident[:, :])
                last.then_inc(s["pT_psum"], 1)

            def readout(b, c0, n):
                if c0 == 0 and b:
                    pe.wait_ge(s["x1_ready"], b)
                for c in range(c0, c0 + n):
                    j = c // 4
                    if c % 4 == 0:
                        pT_copied(pe, b, j)
                        pe.wait_ge(ld_ctxN[b][j // 2], 16)
                    last = t_.matmul(ro_ps, pT_sb[:, c, :], ctxN_sb(b)[:, c, :],
                                     start=(c == 0), stop=(c == 4 * KB - 1))
                if c0 + n == 4 * KB:
                    last.then_inc(s["readout_ready"], 1)

            def in_proj(b, half):
                if half == 0:
                    xT(1, b)
                    pe.wait_ge(xT_ready, B + b + 1)
                    pe.wait_ge(ld_inw, 16)
                    if b:
                        bc_copied(pe, b - 1, NBC)
                dst, ready = ((h_ps, "h_ready"), (gate_ps, "gate_ready"))[half]
                for i in range(CT):
                    for c in range(KD):
                        lo = half * C + i * P
                        last = t_.matmul(dst[:, i * T:(i + 1) * T], inw_sb[:, c, lo:lo + P],
                                         xT_sb[:, b, c, :], start=(c == 0), stop=(c == KD - 1))
                last.then_inc(s[ready], 1)

            def x_proj(b):
                if not b:
                    pe.wait_ge(xT_ready, B)
                pe.wait_ge(s["u_ready"], b + 1)
                pe.wait_ge(ld_xw, 16)
                for i in range(CT):
                    last = t_.matmul(xp_ps, u_sb[:, b, i, :], xw_sb[:, i, :], start=(i == 0), stop=(i == CT - 1))
                last.then_inc(s["xp_ready"], 1)

            def turn_dt(b):
                pe.wait_ge(s["dtn_ready"], b + 1)
                pe.wait_ge(s["sg_ready"], b + 1)
                t_.transpose(dtT_ps, dtn[:, :], ident[:, :]).then_inc(s["dtT_psum"], 1)

            def turn_parts(b):
                pe.wait_ge(s["part2"], b + 1)
                pe.wait_ge(s["ident_bf_ready"], 1)
                pe.wait_ge(s["dtT_ready"], b + 1)
                t_.transpose(partsT_ps, parts[:, :, :, :].rearrange("p a b n -> p (a b n)"),
                             ident_bf[:, :]).then_inc(s["partsT_psum"], 1)

            def dt_proj(b):
                pe.wait_ge(s["dtT_ready"], b + 1)
                pe.wait_ge(ld_dtw, 16)
                for i in range(CT):
                    last = t_.matmul(z_ps[:, i * T:(i + 1) * T], dtw_sb[:, i * P:(i + 1) * P], dtT[:, :],
                                     start=True, stop=True)
                last.then_inc(s["z_psum"], 1)

            def spread(b, j):
                if j == 0:
                    pe.wait_ge(s["partsT_ready"], b + 1)
                    pe.wait_ge(s["pick_ready"], 1)
                if j == 1:
                    pe.wait_ge(s["z_ready"], b + 1)
                if j >= 2:
                    pe.wait_ge(s["bc_odd" if j % 2 else "bc_even"], NBC // 2 * b + j // 2)
                for q in range(4):
                    n = 4 * j + q
                    last = t_.matmul(bc_ps[j % 2][:, q * T:(q + 1) * T],
                                     pick[:, n:n + 1].to_broadcast([3 * 2 * N, P]), partsT[:, :],
                                     start=True, stop=True)
                last.then_inc(s["bc_psum"], 1)

            def sum_states(m):
                times_c_done(pe, m)
                for n in range(NH):
                    last = t_.matmul(work[:, m // 2, 0:T], ident[:, :], st[:, m % 4, n, :],
                                     start=(m % 2 == 0 and n == 0), stop=(m % 2 == 1 and n == NH - 1))
                last.then_inc(s["y_psum"], 1)

            def out_proj(b):
                pe.wait_ge(s["yg_ready"], CT * (b + 1))
                pe.wait_ge(s["x1_ready"], B)
                pe.wait_ge(ld_outw, 16)
                for i in range(CT):
                    last = t_.matmul(op_ps, sg_sb[:, b, i, :], outw_sb[:, i, :], start=(i == 0), stop=(i == CT - 1))
                last.then_inc(s["op_ready"], 1)

            def router(b):
                pe.wait_ge(xT_ready, 2 * B + b + 1)
                pe.wait_ge(ld_gw, 16)
                for c in range(KD):
                    last = t_.matmul(lg_ps, xT_sb[:, b, c, :], gw_sb[:, c, :], start=(c == 0), stop=(c == KD - 1))
                last.then_inc(s["lg_ready"], 1)

            def gate_up(b, p, *es):
                pe.wait_ge(ld_ffn[p], 48)
                for e in es or range(2):
                    k = 2 * (PAIRS * b + p) + e
                    if k >= 4:
                        gate_up_used(pe, k - 4)
                    else:
                        pe.wait_ge(s["yg_ready"], CT)
                    if b:
                        pe.wait_ge(s["lo_dve"], p + 1)
                        pe.wait_ge(s["lo_pool"], p + 1)
                        pe.wait_ge(s["x_lo_ready"], 1)
                        for c in range(KD):
                            at = (2 * c + e) * 2 * I
                            w_hi = w13_hi[:, p % 3, at:at + 2 * I]
                            w_lo = w13_lo[:, p % 2, at:at + 2 * I]
                            xh, xl = x_hi[:, c * T:(c + 1) * T], x_lo[:, c * T:(c + 1) * T]
                            for x_part, w_part in ((xh, w_hi), (xh, w_lo), (xl, w_hi)):
                                last = t_.matmul(work[:, k % 4, 0:2 * I], x_part, w_part,
                                                 start=(c == 0 and w_part is w_hi and x_part is xh),
                                                 stop=(c == KD - 1 and x_part is xl))
                    else:
                        for c in range(KD):
                            last = t_.matmul(work[:, k % 4, 0:2 * I], xT_sb[:, b, c, :], w13_sb(p)[:, c, e, :],
                                             start=(c == 0), stop=(c == KD - 1))
                    last.then_inc(s["gu_ready"], 1)

            def turn_h(b, p):
                k = PAIRS * b + p
                gate_used(pe, 2 * k + 1)
                src = h_sb[:, p % 2] if b else h0_sb[:, p % 3]
                if k:
                    pe.wait_ge(s["hT_ready"], 2 * k)
                for c, (lo, m) in enumerate(HC):
                    last = t_.transpose(tr_ps[0:m, c * P:c * P + T], src[:, lo:lo + m], ident[:, :])
                last.then_inc(s["tr_ready"], 1)

            def down(b, p):
                k = PAIRS * b + p
                pe.wait_ge(s["hT_ready"], 2 * k + 2)
                pe.wait_ge(ld_ffn[p], 48)
                if p == 0 and b:
                    pe.wait_ge(s["fin_ready"], b)
                for c, (lo, m) in enumerate(HC):
                    last = t_.matmul(acc_ps[:, b * D:(b + 1) * D], hT[0:m, k % 2, c * P:(c + 1) * P],
                                     w2_sb(p)[0:m, c, :], start=(p == 0 and c == 0),
                                     stop=(p == PAIRS - 1 and c == 2))
                last.then_inc(s["w2_done"], 1)

            pe.wait_ge(s["ident_ready"], 1)
            warm_up(9, ident[:, :], acc_ps)
            xT(0, 0)
            warm_up(2, ident[:, :], acc_ps)
            for j in range(4):
                scores(0, j)
            xT(0, 1)
            warm_up(8, ident[:, :], acc_ps)
            for j in range(3):
                transposes(0, j)
            readout(0, 0, 2)
            transposes(0, 3)
            for c in range(2, 16, 2):
                readout(0, c, 2)
            scores(1, 0)
            in_proj(0, 0)
            scores(1, 1)
            in_proj(0, 1)
            scores(1, 2)
            scores(1, 3)
            x_proj(0)
            transposes(1, 0)
            turn_dt(0)
            transposes(1, 1)
            transposes(1, 2)
            dt_proj(0)
            turn_parts(0)
            transposes(1, 3)
            spread(0, 0)
            readout(1, 0, 2)
            spread(0, 1)
            readout(1, 2, 2)
            spread(0, 2)
            spread(0, 3)
            for c in range(4, 10, 2):
                readout(1, c, 2)
            spread(0, 4)
            spread(0, 5)
            for c in range(10, 16, 2):
                readout(1, c, 2)
            warm_up(4, inw_sb[:, 0, 0:D], work[:, 3])
            spread(0, 6)
            spread(0, 7)
            warm_up(4, ident[:, :], work[:, 3])
            in_proj(1, 0)
            in_proj(1, 1)
            sum_states(0)
            sum_states(1)
            x_proj(1)
            sum_states(2)
            turn_dt(1)
            warm_up(4, ident[:, :], work[:, 3])
            turn_parts(1)
            dt_proj(1)
            spread(1, 0)
            sum_states(3)
            for j in range(1, 4):
                spread(1, j)
            sum_states(4)
            spread(1, 4)
            spread(1, 5)
            sum_states(5)
            sum_states(6)
            spread(1, 6)
            sum_states(7)
            spread(1, 7)
            out_proj(0)
            warm_up(13, ident[:, :], work[:, 3])
            xT(2, 0)
            router(0)
            gate_up(0, 0, 0)
            gate_up(0, 0, 1)
            gate_up(0, 1, 0)
            gate_up(0, 1, 1)
            gate_up(0, 2, 0)
            turn_h(0, 0)
            gate_up(0, 2, 1)
            down(0, 0)
            turn_h(0, 1)
            gate_up(0, 3, 0)
            gate_up(0, 3, 1)
            gate_up(0, 4, 0)
            down(0, 1)
            turn_h(0, 2)
            gate_up(0, 4, 1)
            gate_up(0, 5, 0)
            gate_up(0, 5, 1)
            turn_h(0, 3)
            down(0, 2)
            gate_up(0, 6, 0)
            down(0, 3)
            turn_h(0, 4)
            gate_up(0, 6, 1)
            turn_h(0, 5)
            gate_up(0, 7, 0)
            gate_up(0, 7, 1)
            down(0, 4)
            down(0, 5)
            out_proj(1)
            turn_h(0, 6)
            gate_up(0, 8, 0)
            gate_up(0, 8, 1)
            turn_h(0, 7)
            xT(2, 1)
            down(0, 6)
            down(0, 7)
            router(1)
            turn_h(0, 8)
            gate_up(1, 0, 0)
            down(0, 8)
            gate_up(1, 0, 1)
            for p in range(1, PAIRS):
                gate_up(1, p, 0)
                turn_h(1, p - 1)
                gate_up(1, p, 1)
                down(1, p - 1)
            turn_h(1, PAIRS - 1)
            down(1, PAIRS - 1)

def kernel(**inputs):
    import numpy as np
    import concourse.bacc as bacc
    from concourse.bass_utils import run_bass_kernel_spmd as run

    a = {k: np.asarray(v) for k, v in inputs.items()}
    C = a["L0_attn_out_proj_w"].shape[0]
    chan = np.concatenate([a["L0_attn_conv_w"][:, 0, :], a["L0_attn_conv_b"][:, None],
                           a["L0_attn_dt_proj_b"][:, None], a["L0_attn_D_param"][:, None],
                           a["L0_attn_A_log"]], axis=1)
    chan = chan.reshape(C // 128, 128, -1).transpose(1, 0, 2)
    E, I2, D = a["L0_ffn_w13"].shape
    I = I2 // 2
    sw13 = a["L0_ffn_sw13"].reshape(2, 2, I, D).transpose(1, 0, 2, 3).reshape(2, I2, D)
    w13 = np.concatenate([a["L0_ffn_w13"], sw13], axis=0).reshape(-1, 2, I2, D).transpose(0, 3, 1, 2)
    w2 = np.concatenate([a["L0_ffn_w2"].transpose(0, 2, 1).reshape(-1, D), a["L0_ffn_sw2"].T], axis=0)
    arrays = {
        "x": a["x"], "ctx_t": a["ctx_2048"].transpose(0, 2, 1), "ctx_n": a["ctx_2048"],
        "mask": a["mask_BxS2_bk0"].reshape(1, -1), "in_w": a["L0_attn_in_proj_w"], "chan": chan,
        "x_w": a["L0_attn_x_proj_w"], "dt_w": a["L0_attn_dt_proj_w"], "out_w": a["L0_attn_out_proj_w"],
        "gate_w": a["L0_ffn_gate_w"].T, "w13": w13, "w2": w2,
    }
    arrays = {k: np.ascontiguousarray(v) for k, v in arrays.items()}
    nc = bacc.Bacc("TRN2", target_bir_lowering=False, num_devices=1)
    args = [nc.dram_tensor(f"in_{k}", v.shape, mybir.dt.from_np(v.dtype), kind="ExternalInput").ap()
            for k, v in arrays.items()]
    out = nc.dram_tensor("out_0", a["x"].shape, F32, kind="ExternalOutput").ap()
    build(nc, *args, out)
    r = run(nc, [{f"in_{k}": v for k, v in arrays.items()}], core_ids=[0])
    return r.results[0]["out_0"]
```
